# Optimizing a Trainium2 kernel written in Bass

```python
import numpy as np
import jax
import jax.numpy as jnp

def _softmax(x, axis=-1):
    return jax.nn.softmax(x, axis=axis)

def _gelu(x):
    return jax.nn.gelu(x, approximate=True)

def _silu(x):
    return jax.nn.silu(x)

def _sigmoid(x):
    return jax.nn.sigmoid(x)

def _layernorm(x, axis=-1, eps=1e-05):
    m = jnp.mean(x, axis=axis, keepdims=True)
    v = jnp.var(x, axis=axis, keepdims=True)
    return (x - m) / jnp.sqrt(v + eps)

def _scatter_add(tgt, idx, src, axis=0):
    return tgt.at[idx].add(src)

def _segment_sum(src, seg, n):
    return jax.ops.segment_sum(src, seg, n)
kernel_name = 'mk_cond_resid_d4_seqx_r4_4f458f'

def setup_inputs(seed: int=0):
    np.random.seed(seed)
    _w = jnp.asarray

    def _rec_inputs():
        import jax
        import jax.numpy as jnp
        _rk = jax.random.key(seed)
        x = 0.5 + 0.2887 * jax.random.normal(jax.random.fold_in(_rk, 1), (2, 1024, 256), jnp.float32)
        _lenS = 1024 - jax.random.randint(jax.random.fold_in(_rk, 7), (2,), 0, max(1, 1024 // 4) + 1, jnp.int32)
        _lenS2 = 1024 - jax.random.randint(jax.random.fold_in(_rk, 8), (2,), 0, max(1, 1024 // 4) + 1, jnp.int32)
        condB_zX = jax.random.uniform(jax.random.fold_in(_rk, 11), (2,), jnp.float32, 0.0, 0.983423)
        condB_zY = jax.random.uniform(jax.random.fold_in(_rk, 12), (2,), jnp.float32, 0.0, 0.979075)
        condB_zR = jax.random.uniform(jax.random.fold_in(_rk, 13), (2,), jnp.float32, 0.0, 0.9968)
        itok_B_0_2 = jax.random.randint(jax.random.fold_in(_rk, 14), (2,), 0, 3, jnp.int32)
        itok_B_0_15 = jax.random.randint(jax.random.fold_in(_rk, 15), (2,), 0, 16, jnp.int32)
        fside_Bx8_0 = jax.random.uniform(jax.random.fold_in(_rk, 16), (2, 8), jnp.float32, 0.0, 0.556406)
        condB_sharedgateprob = jax.random.uniform(jax.random.fold_in(_rk, 17), (2,), jnp.float32, 0.0, 0.794948)
        return (x, condB_zX, condB_zY, condB_zR, itok_B_0_2, itok_B_0_15, fside_Bx8_0, condB_sharedgateprob)
    x, condB_zX, condB_zY, condB_zR, itok_B_0_2, itok_B_0_15, fside_Bx8_0, condB_sharedgateprob = _rec_inputs()

    def _L0_cond_setup():
        import jax, jax.numpy as jnp
        import numpy as np
        key = jax.random.key(seed)
        k1, k2, k3, k4 = jax.random.split(key, 4)
        B, H, W = (64, 256, 256)
        return {'y': jax.random.uniform(k1, (B, H, W), dtype=jnp.float32), 'zX': jax.random.uniform(k2, (B, 1), dtype=jnp.float32), 'zY': jax.random.uniform(k3, (B, 1), dtype=jnp.float32), 'zR': jax.random.uniform(k4, (B, 1), dtype=jnp.float32), 'dx': 1, 'dy': 1}
    _L0_cond_all = _L0_cond_setup()
    _L0_cond_in = {k: v for k, v in _L0_cond_all.items() if k in ()}
    del _L0_cond_all

    def _L1_cond_setup():
        import jax, jax.numpy as jnp
        import numpy as np
        NEG_INF = -1e+30
        key = jax.random.key(seed)
        k1, k2, k3, k4, k5 = jax.random.split(key, 5)
        B, S, D, A = (16, 256, 256, 64)
        hidden = jax.random.normal(k1, (B, S, D), dtype=jnp.float32)
        W1 = jax.random.normal(k2, (D, A), dtype=jnp.float32) / np.sqrt(D)
        b1 = jax.random.normal(k3, (A,), dtype=jnp.float32) * 0.01
        v = jax.random.normal(k4, (A,), dtype=jnp.float32) / np.sqrt(A)
        prompt_type_ids = jax.random.randint(k5, (B,), 0, 3, dtype=jnp.int32)
        return {'hidden': hidden, 'W1': W1, 'b1': b1, 'v': v, 'prompt_type_ids': prompt_type_ids}
    _L1_cond_all = _L1_cond_setup()
    _L1_cond_in = {k: v for k, v in _L1_cond_all.items() if k in ('W1', 'b1', 'v')}
    del _L1_cond_all

    def _L2_cond_setup():
        import jax, jax.numpy as jnp
        import numpy as np
        B, N, DIM = (32, 256, 256)
        HID = 1024
        PART = 64
        OUT = 256
        SHARED = OUT - PART
        E = 16
        key = jax.random.key(seed)
        ks = jax.random.split(key, 8)
        s = 0.02
        return {'x': jax.random.normal(ks[0], (B, N, DIM), dtype=jnp.float32), 'indices': jax.random.randint(ks[1], (B,), 0, E, dtype=jnp.int64), 'fc1_w': jax.random.normal(ks[2], (HID, DIM), dtype=jnp.float32) * s, 'fc1_b': jnp.zeros((HID,), dtype=jnp.float32), 'fc2_w': jax.random.normal(ks[3], (SHARED, HID), dtype=jnp.float32) * s, 'fc2_b': jnp.zeros((SHARED,), dtype=jnp.float32), 'experts_w': jax.random.normal(ks[4], (E, PART, HID), dtype=jnp.float32) * s, 'experts_b': jnp.zeros((E, PART), dtype=jnp.float32)}
    _L2_cond_all = _L2_cond_setup()
    _L2_cond_in = {k: v for k, v in _L2_cond_all.items() if k in ('fc1_w', 'fc1_b', 'fc2_w', 'fc2_b', 'experts_w', 'experts_b')}
    del _L2_cond_all

    def _L3_cond_setup():
        import jax, jax.numpy as jnp
        import numpy as np
        E, B, S, D, F = (8, 2, 256, 256, 1024)
        key = jax.random.key(seed)
        ks = jax.random.split(key, 9)
        sc_d = 1.0 / np.sqrt(D)
        sc_f = 1.0 / np.sqrt(F)
        hidden_states = jax.random.normal(ks[0], (B, S, D), dtype=jnp.float32)
        gating_probs = jax.nn.softmax(jax.random.normal(ks[1], (B, E), dtype=jnp.float32), axis=-1)
        shared_gate_prob = jax.nn.sigmoid(jax.random.normal(ks[2], (B, 1), dtype=jnp.float32))
        Wg = jax.random.normal(ks[3], (E, D, F), dtype=jnp.float32) * sc_d
        Wu = jax.random.normal(ks[4], (E, D, F), dtype=jnp.float32) * sc_d
        Wd = jax.random.normal(ks[5], (E, F, D), dtype=jnp.float32) * sc_f
        Sg = jax.random.normal(ks[6], (D, F), dtype=jnp.float32) * sc_d
        Su = jax.random.normal(ks[7], (D, F), dtype=jnp.float32) * sc_d
        Sd = jax.random.normal(ks[8], (F, D), dtype=jnp.float32) * sc_f
        return {'hidden_states': hidden_states, 'gating_probs': gating_probs, 'shared_gate_prob': shared_gate_prob, 'Wg': Wg, 'Wu': Wu, 'Wd': Wd, 'Sg': Sg, 'Su': Su, 'Sd': Sd}
    _L3_cond_all = _L3_cond_setup()
    _L3_cond_in = {k: v for k, v in _L3_cond_all.items() if k in ('Wg', 'Wu', 'Wd', 'Sg', 'Su', 'Sd')}
    del _L3_cond_all
    return {'x': x, 'condB_zX': condB_zX, 'condB_zY': condB_zY, 'condB_zR': condB_zR, 'itok_B_0_2': itok_B_0_2, 'itok_B_0_15': itok_B_0_15, 'fside_Bx8_0': fside_Bx8_0, 'condB_sharedgateprob': condB_sharedgateprob, 'L1_cond_W1': _L1_cond_in['W1'], 'L1_cond_b1': _L1_cond_in['b1'], 'L1_cond_v': _L1_cond_in['v'], 'L2_cond_fc1_w': _L2_cond_in['fc1_w'], 'L2_cond_fc1_b': _L2_cond_in['fc1_b'], 'L2_cond_fc2_w': _L2_cond_in['fc2_w'], 'L2_cond_fc2_b': _L2_cond_in['fc2_b'], 'L2_cond_experts_w': _L2_cond_in['experts_w'], 'L2_cond_experts_b': _L2_cond_in['experts_b'], 'L3_cond_Wg': _L3_cond_in['Wg'], 'L3_cond_Wu': _L3_cond_in['Wu'], 'L3_cond_Wd': _L3_cond_in['Wd'], 'L3_cond_Sg': _L3_cond_in['Sg'], 'L3_cond_Su': _L3_cond_in['Su'], 'L3_cond_Sd': _L3_cond_in['Sd']}

def reference(x, condB_zX, condB_zY, condB_zR, itok_B_0_2, itok_B_0_15, fside_Bx8_0, condB_sharedgateprob, L1_cond_W1, L1_cond_b1, L1_cond_v, L2_cond_fc1_w, L2_cond_fc1_b, L2_cond_fc2_w, L2_cond_fc2_b, L2_cond_experts_w, L2_cond_experts_b, L3_cond_Wg, L3_cond_Wu, L3_cond_Wd, L3_cond_Sg, L3_cond_Su, L3_cond_Sd):
    import jax
    import jax.numpy as jnp

    def _L0_cond_ref(y, zX, zY, zR, dx, dy):
        import jax, jax.numpy as jnp
        import numpy as np
        yp_x = jnp.pad(y, ((0, 0), (0, 0), (1, 1)), mode='reflect')
        lap_x = (yp_x[:, :, :-2] - 2.0 * y + yp_x[:, :, 2:]) / (dx * dx)
        yp_y = jnp.pad(y, ((0, 0), (1, 1), (0, 0)), mode='reflect')
        lap_y = (yp_y[:, :-2, :] - 2.0 * y + yp_y[:, 2:, :]) / (dy * dy)
        du_dt = zX[:, :, None] * lap_x + zY[:, :, None] * lap_y + zR[:, :, None] * y * (1.0 - y)
        return du_dt

    def _L1_cond_ref(hidden, W1, b1, v, prompt_type_ids):
        import jax, jax.numpy as jnp
        import numpy as np
        NEG_INF = -1e+30
        B, S, D = hidden.shape
        attn_in = jnp.tanh(jnp.einsum('bsd,da->bsa', hidden, W1) + b1)
        scores = jnp.einsum('bsa,a->bs', attn_in, v)
        idx = jnp.arange(S)
        j = idx[:, None]
        l = idx[None, :]
        prefix_m = l <= j
        postfix_m = l >= j
        cloze_m = l != j
        pt = prompt_type_ids[:, None, None]
        mask = jnp.where(pt == 0, prefix_m[None], jnp.where(pt == 1, postfix_m[None], cloze_m[None]))
        masked_scores = jnp.where(mask, scores[:, None, :], NEG_INF)
        p = jax.nn.softmax(masked_scores, axis=-1)
        cnt = jnp.sum(mask, axis=-1).astype(hidden.dtype)
        pooled = jnp.einsum('bjl,bld->bjd', p, hidden) / cnt[..., None]
        return pooled

    def _L2_cond_ref(x, indices, fc1_w, fc1_b, fc2_w, fc2_b, experts_w, experts_b):
        import jax, jax.numpy as jnp
        import numpy as np
        B, N, DIM = (32, 256, 256)
        HID = 1024
        PART = 64
        OUT = 256
        SHARED = OUT - PART
        E = 16
        h = jax.nn.gelu(jnp.einsum('bnd,hd->bnh', x, fc1_w) + fc1_b, approximate=False)
        shared = jnp.einsum('bnh,sh->bns', h, fc2_w) + fc2_b
        We = experts_w[indices]
        be = experts_b[indices]
        expert_x = jnp.einsum('bnh,bph->bnp', h, We) + be[:, None, :]
        return jnp.concatenate([shared, expert_x], axis=-1)

    def _L3_cond_ref(hidden_states, gating_probs, shared_gate_prob, Wg, Wu, Wd, Sg, Su, Sd):
        import jax, jax.numpy as jnp
        import numpy as np
        E, B, S, D, F = (8, 2, 256, 256, 1024)
        h = hidden_states
        g = jnp.einsum('bsd,edf->ebsf', h, Wg)
        u = jnp.einsum('bsd,edf->ebsf', h, Wu)
        expert_outs = jnp.einsum('ebsf,efd->ebsd', jax.nn.silu(g) * u, Wd)
        expert_output = jnp.einsum('be,ebsd->bsd', gating_probs, expert_outs)
        shared = jnp.einsum('bsf,fd->bsd', jax.nn.silu(h @ Sg) * (h @ Su), Sd)
        sg = shared_gate_prob[:, :, None]
        return (1.0 - sg) * expert_output + sg * shared
    x = x + _L0_cond_ref(x, condB_zX[:, None], condB_zY[:, None], condB_zR[:, None], 1, 1)
    x = x + _L1_cond_ref(x, L1_cond_W1, L1_cond_b1, L1_cond_v, itok_B_0_2)
    x = x + _L2_cond_ref(x, itok_B_0_15, L2_cond_fc1_w, L2_cond_fc1_b, L2_cond_fc2_w, L2_cond_fc2_b, L2_cond_experts_w, L2_cond_experts_b)
    x = x + _L3_cond_ref(x, fside_Bx8_0, condB_sharedgateprob[:, None], L3_cond_Wg, L3_cond_Wu, L3_cond_Wd, L3_cond_Sg, L3_cond_Su, L3_cond_Sd)
    return x

_drawn_inputs = setup_inputs


def setup_inputs(seed=0):
    import zlib

    import numpy as np

    out = dict(_drawn_inputs(seed))
    spreads = {'L2_cond_fc1_b': (0.0, 0.1), 'L2_cond_fc2_b': (0.0, 0.1), 'L2_cond_experts_b': (0.0, 0.1)}
    factors = {}
    for name, (base, spread) in spreads.items():
        noise = np.random.default_rng([zlib.crc32(name.encode()), seed]).standard_normal(out[name].shape)
        drawn = base * np.exp(spread * noise) if base else spread * noise
        out[name] = jnp.asarray(drawn.astype(out[name].dtype))
    for name, factor in factors.items():
        out[name] = (out[name] * factor).astype(out[name].dtype)
    return out
```

```python
import concourse.bass as bass
from concourse import mybir
from contextlib import ExitStack


def stencil_attention_experts(nc, x_rows, scalars, types, expert_ids, w1, b1, v, fc1_w, fc1_b, fc2_w, fc2_b,
                              experts_w, experts_b, moe_w, out):
    f32 = mybir.dt.float32
    f32r = mybir.dt.float32r
    i32 = mybir.dt.int32
    ALU = mybir.AluOpType
    ACT = mybir.ActivationFunctionType
    AX = mybir.AxisListType.X

    P = 128
    B, S = x_rows.shape[1:]
    D = x_rows.shape[0] - 2
    DC = D // P
    T = B * S
    TB = 512
    NT = T // TB
    NTB = S // TB
    A = w1.shape[1]
    F = fc1_b.shape[0] * fc1_b.shape[1]
    FC = F // P
    KC = S // P
    E = moe_w.shape[0]
    EG = E - 1
    WE = moe_w.shape[2]
    WQ = WE // NT
    PIECES = FC // 2
    WP = WQ // PIECES
    UP = DC * F
    SHARED = fc2_w.shape[2]
    NEG = -1e30
    PAIR = 2
    RING = 4
    ds = bass.ds

    with ExitStack() as ctx:
        def sb(name, shape, dt=f32):
            return ctx.enter_context(nc.sbuf_tensor(name, shape, dt))

        def sem(name):
            return ctx.enter_context(nc.semaphore(name))

        xT = sb("xT", [P, DC, T])
        x_hi = sb("x_hi", [P, DC, T], f32r)
        x_lo = sb("x_lo", [P, DC, T], f32r)
        raw = sb("raw", [P, WE])
        w_hi = [sb("w_hi0", [P, WE], f32r)]
        w_lo = [sb("w_lo0", [P, WE], f32r)]
        ident = sb("ident", [P, P])
        ones = sb("ones", [P, P])
        NB = P + KC * KC + KC
        blend_src = sb("blend_src", [P, 3, NB])
        blend = sb("blend", [P, B, NB])
        same_chunk = sb("same_chunk", [P, KC, KC])
        sc_in = sb("sc_in", [P, scalars.shape[0]])
        type_i = sb("type_i", [P, B], i32)
        type_f = sb("type_f", [P, B])
        sel = sb("sel", [P, 3, B])
        ids = sb("ids", [1, B], i32)
        c0 = sb("c0", [P, B])
        neg_zr = sb("neg_zr", [P, B])
        one_less_sg = sb("one_less_sg", [P, B])
        gate = sb("gate", [P, E, NT])
        w1_sb = sb("w1_sb", [P, DC, A])
        b1_sb = sb("b1_sb", [A, 1])
        v_sb = sb("v_sb", [A, 1])
        v_wide = sb("v_wide", [A, P])
        fc1_bias = sb("fc1_bias", [P, FC])
        out_bias = sb("out_bias", [P, B, DC])
        inner_max = sb("inner_max", [P, B, KC])
        chunk_max = sb("chunk_max", [P, B, KC])
        flagged = sb("flagged", [P, B, KC, KC])
        outer_max = sb("outer_max", [P, B, KC])
        row_max = sb("row_max", [P, B, KC])
        exp_in = sb("exp_in", [P, B, KC * KC + KC])
        exp_out = sb("exp_out", [P, B, KC * KC + KC])
        denom = sb("denom", [P, B, KC])
        outer_sum = sb("outer_sum", [P, B, KC])
        recip = sb("recip", [P, B, KC])
        outer_w = sb("outer_w", [P, B, KC])
        outer_diag = sb("outer_diag", [P, B, KC, KC])
        ctx_sb = sb("ctx_sb", [KC, B, D])

        with ExitStack() as early:
            def eb(name, shape, dt=f32):
                return early.enter_context(nc.sbuf_tensor(name, shape, dt))
            x_pad = eb("x_pad", [P, B, DC, S + 2])
            x_up = eb("x_up", [P, B, DC, S])
            x_dn = eb("x_dn", [P, B, DC, S])
            poly = eb("poly", [P, B, DC, S])
        x_tok = x_up[:, :, :, :].rearrange("p b c (h s) -> p b (c h) s", s=D)
        attn = x_dn[0:A, :, 0, :]
        probs = x_dn[:, :, 1, :].rearrange("p b (k l) -> p b k l", l=P)
        probs_t = poly[:, :, 0, :].rearrange("p b (k l) -> p b k l", l=P)
        outer_t = poly[0:KC, :, 1, :]
        w_hi.append(sb("w_hi1", [P, WE], f32r))
        w_lo.append(sb("w_lo1", [P, WE], f32r))
        stage = sb("stage", [P, PAIR, TB])
        hidden = sb("hidden", [P, PAIR, TB])
        h_hi = sb("h_hi", [P, RING, TB], f32r)
        h_lo = sb("h_lo", [P, RING, TB], f32r)

        ps = ctx.enter_context(nc.psum_tensor("ps", [P, 8, TB], f32))
        OUT = 4

        consts_done = sem("consts_done")
        scal_in = sem("scal_in")
        types_in = sem("types_in")
        ids_in = sem("ids_in")
        w1_in = sem("w1_in")
        bias_in = sem("bias_in")
        x_in = [sem(f"x_in{b}") for b in range(B)]
        fc_in = sem("fc_in")
        raw_in = [sem(f"raw_in{q}") for q in range(NT)]
        dve_step = sem("dve_step")
        coef_done = sem("coef_done")
        pool_step = sem("pool_step")
        edges_done = sem("edges_done")
        rows_summed = sem("rows_summed")
        poly_done = sem("poly_done")
        x1_done = sem("x1_done")
        attn_ps = sem("attn_ps")
        attn_done = sem("attn_done")
        scores_ps = sem("scores_ps")
        cols_ps = sem("cols_ps")
        tok_ps = sem("tok_ps")
        tok_done = sem("tok_done")
        scores_read = sem("scores_read")
        exps_asked = sem("exps_asked")
        exps_done = sem("exps_done")
        probs_asked = sem("probs_asked")
        probs_done = sem("probs_done")
        outer_ps = sem("outer_ps")
        outer_read = sem("outer_read")
        ctx_ps = sem("ctx_ps")
        ctx_done = sem("ctx_done")
        probs_scaled = sem("probs_scaled")
        probst_ps = sem("probst_ps")
        probst_done = sem("probst_done")
        outert_ps = sem("outert_ps")
        outert_done = sem("outert_done")
        pooled_ps = sem("pooled_ps")
        x2_done = sem("x2_done")
        fc_split = sem("fc_split")
        fc_up = sem("fc_up")
        gelu_done = sem("gelu_done")
        fc_h_ready = sem("fc_h_ready")
        down_done = sem("down_done")
        out_ready = sem("out_ready")
        out_free = sem("out_free")
        x3_done = sem("x3_done")
        hi_done = sem("hi_done")
        up_done = sem("up_done")
        silu_done = sem("silu_done")
        mul_done = sem("mul_done")
        h_ready = sem("h_ready")
        whi_done = sem("whi_done")
        wlo_done = sem("wlo_done")
        stored = sem("stored")

        ZX, ZY, ZR, SG, GP = 0, B, 2 * B, 3 * B, 4 * B
        block = ctx.enter_context(nc.Block())

        FC2 = [UP] * B
        FC2B = [UP + FC * P * (1 + b) for b in range(B)]
        FCW = UP + FC * P * (1 + B)

        def fc2_cols(tile, b, c):
            at = FC2[b] if c == 0 else FC2B[b]
            return tile[:, at:at + FC * P].rearrange("p (k m) -> p k m", m=P)

        @block.sync
        def _(sp):
            for b in range(B):
                for tile, shift in ((x_pad[:, b, :, 1:S + 1], 1), (x_up[:, b], 2), (x_dn[:, b], 0)):
                    sp.dma_start(tile, x_rows[shift:shift + D, b, :].rearrange("(c p) s -> p c s", p=P)) \
                      .then_inc(x_in[b], 16)
            sp.dma_start(raw[:, 0:UP].rearrange("p (c f) -> p c f", c=DC), fc1_w).then_inc(fc_in, 16)
            sp.dma_start(fc2_cols(raw, 0, 0), fc2_w[:, :, 0:P]).then_inc(fc_in, 16)
            sp.wait_ge(ids_in, 16)
            for b in range(B):
                sp.dma_start(fc2_cols(raw, b, 1)[:, :, 0:SHARED - P], fc2_w[:, :, P:SHARED]).then_inc(fc_in, 16)
                eid = sp.value_load(ids[0:1, b:b + 1], min_val=0, max_val=experts_w.shape[0] - 1)
                sp.dma_start(fc2_cols(raw, b, 1)[:, :, SHARED - P:P],
                             experts_w[ds(eid, 1), :, :, :].rearrange("e p k m -> (e p) k m")).then_inc(fc_in, 16)
                sp.dma_start(out_bias[SHARED - P:P, b, 1:2],
                             experts_b[ds(eid, 1), :].rearrange("e m -> m e")).then_inc(bias_in, 16)
            sp.wait_ge(fc_split, 1)
            for q in range(NT):
                sp.dma_start(raw[:, q * WQ:(q + 1) * WQ], moe_w[0, :, q * WQ:(q + 1) * WQ]).then_inc(raw_in[q], 16)
            with sp.Fori(1, E) as e:
                for q in range(NT):
                    sp.wait_ge(wlo_done, (e - 1) * (NT * PIECES) + (q + 1) * PIECES)
                    sp.dma_start(raw[:, q * WQ:(q + 1) * WQ],
                                 moe_w[ds(e, 1), :, q * WQ:(q + 1) * WQ].rearrange("e p w -> (e p) w")) \
                      .then_inc(raw_in[q], 16)
            for t in range(NT):
                sp.wait_ge(out_free, 1 + NT + (E - 1) * NT + t + 1)
                sp.dma_start(out.rearrange("(c p) t -> p c t", p=P)[:, :, t * TB:(t + 1) * TB],
                             xT[:, :, t * TB:(t + 1) * TB]).then_inc(stored, 16)
            sp.wait_ge(stored, 16 * NT)

        @block.gpsimd
        def _(pool):
            steps = [0]

            def link(ins):
                steps[0] += 1
                ins.then_inc(pool_step, 1)
                pool.wait_ge(pool_step, steps[0])

            nc.gpsimd.memset(ident[:, :], 0.0).then_inc(pool_step, 1)
            nc.gpsimd.memset(ones[:, :], 1.0).then_inc(pool_step, 1)
            nc.gpsimd.memset(same_chunk[:, :, :], 0.0).then_inc(pool_step, 1)
            nc.gpsimd.memset(blend_src[:, :, :], 0.0).then_inc(pool_step, 1)
            steps[0] = 4
            pool.wait_ge(pool_step, 4)
            masks = [blend_src[:, i, 0:P] for i in range(3)]
            flags = [blend_src[:, i, P:P + KC * KC].rearrange("p (k c) -> p k c", c=KC) for i in range(3)]
            counts = [blend_src[:, i, P + KC * KC:NB] for i in range(3)]

            def fill_where(tile, compare, fill, pattern, row):
                return nc.gpsimd.affine_select(out=tile, in_=tile, compare_op=compare, fill=fill, base=0,
                                               pattern=pattern, channel_multiplier=row)

            fill_where(ident[:, :], ALU.not_equal, 1.0, [[-1, P]], 1)
            fill_where(masks[0], ALU.is_ge, NEG, [[-1, P]], 1)
            fill_where(masks[1], ALU.is_ge, NEG, [[1, P]], -1)
            fill_where(masks[2], ALU.not_equal, NEG, [[-1, P]], 1)
            fill_where(flags[0], ALU.is_gt, NEG, [[1, KC], [-1, KC]], 0)
            fill_where(flags[1], ALU.is_gt, NEG, [[-1, KC], [1, KC]], 0)
            fill_where(flags[2], ALU.not_equal, NEG, [[1, KC], [-1, KC]], 0)
            fill_where(same_chunk[:, :, :], ALU.not_equal, 1.0, [[1, KC], [-1, KC]], 0)
            nc.gpsimd.iota(counts[0], [[P, KC]], base=1, channel_multiplier=1, allow_small_or_imprecise_dtypes=True)
            nc.gpsimd.iota(counts[1], [[-P, KC]], base=S, channel_multiplier=-1, allow_small_or_imprecise_dtypes=True)
            nc.gpsimd.memset(counts[2], float(S - 1)).then_inc(consts_done, 1)
            for b in range(B):
                pool.wait_ge(x_in[b], 48)
                nc.gpsimd.tensor_copy(x_pad[:, b, :, 0:1], x_pad[:, b, :, 2:3])
                nc.gpsimd.tensor_copy(x_pad[:, b, :, S + 1:S + 2], x_pad[:, b, :, S - 1:S]).then_inc(edges_done, 1)
                nc.gpsimd.tensor_tensor(x_up[:, b], x_up[:, b], x_dn[:, b], ALU.add).then_inc(rows_summed, 1)
            pool.wait_ge(fc_in, 16 * (2 + 2 * B))
            link(nc.gpsimd.tensor_copy(w_hi[0][:, 0:FCW], raw[:, 0:FCW]))
            nc.gpsimd.tensor_tensor(w_lo[0][:, 0:FCW], raw[:, 0:FCW], w_hi[0][:, 0:FCW].bitcast(f32),
                                    ALU.subtract).then_inc(fc_split, 1)

        @block.scalar
        def _(act):
            act.dma_start(sc_in[:, :], scalars.partition_broadcast(P)).then_inc(scal_in, 16)
            act.dma_start(type_i[:, :], types.partition_broadcast(P)).then_inc(types_in, 16)
            act.dma_start(ids[:, :], expert_ids.unsqueeze(0)).then_inc(ids_in, 16)
            act.dma_start(w1_sb[:, :, :], w1.rearrange("(c p) a -> p c a", p=P)).then_inc(w1_in, 16)
            act.dma_start(b1_sb[:, :], b1.unsqueeze(1)).then_inc(w1_in, 16)
            act.dma_start(v_sb[:, :], v.unsqueeze(1)).then_inc(w1_in, 16)
            act.dma_start(fc1_bias[:, :], fc1_b).then_inc(bias_in, 16)
            for b in range(B):
                act.dma_start(out_bias[:, b, 0:1], fc2_b[0:P].unsqueeze(1)).then_inc(bias_in, 16)
                act.dma_start(out_bias[0:SHARED - P, b, 1:2], fc2_b[P:SHARED].unsqueeze(1)).then_inc(bias_in, 16)
            act.wait_ge(coef_done, 1)
            for b in range(B):
                act.wait_ge(x_in[b], 48)
                nc.scalar.activation(poly[:, b], x_pad[:, b, :, 1:S + 1], ACT.Identity,
                                     bias=c0[:, b:b + 1], scale=neg_zr[:, b:b + 1]).then_inc(poly_done, 1)
            act.wait_ge(w1_in, 48)
            for b in range(B):
                act.wait_ge(attn_ps, b + 1)
                nc.scalar.activation(attn[:, b, :], ps[0:A, 4 * b:4 * b + 2, :].rearrange("p n t -> p (n t)"), ACT.Tanh,
                                     bias=b1_sb[:, 0:1]).then_inc(attn_done, 1)
            for r in range(2):
                for b in range(B):
                    act.wait_ge(tok_ps, 2 * r + b + 1)
                    nc.scalar.activation(x_tok[:, b, r * KC // 2:(r + 1) * KC // 2, :].rearrange("p k d -> p (k d)"),
                                         ps[:, 4 * b + 2:4 * b + 4, :].rearrange("p n t -> p (n t)"),
                                         ACT.Copy).then_inc(tok_done, 1)
            for b in range(B):
                act.wait_ge(exps_asked, b + 1)
                nc.scalar.activation(exp_out[:, b, :], exp_in[:, b, :], ACT.Exp).then_inc(exps_done, 1)
                act.wait_ge(probs_asked, b + 1)
                nc.scalar.activation(probs[:, b], probs[:, b], ACT.Exp).then_inc(probs_done, 1)
            for b in range(B):
                act.wait_ge(ctx_ps, b + 1)
                nc.scalar.activation(ctx_sb[:, b, :], ps[0:KC, 4 * b + 3, 0:D], ACT.Copy).then_inc(ctx_done, 1)
            for b in range(B):
                act.wait_ge(probst_ps, b + 1)
                nc.scalar.activation(probs_t[:, b].rearrange("p k l -> p (k l)"),
                                     ps[:, 4 * b:4 * b + 2, :].rearrange("p n t -> p (n t)"),
                                     ACT.Copy).then_inc(probst_done, 1)
                act.wait_ge(outert_ps, b + 1)
                nc.scalar.activation(outer_t[:, b, :], ps[0:KC, 4 * b + 2:4 * b + 4, :].rearrange("p n t -> p (n t)"),
                                     ACT.Copy).then_inc(outert_done, 1)

            def weight_piece(slot, tb, i, n):
                at = tb * WQ + i * WP
                nc.scalar.activation(w_hi[slot][:, ds(at, WP)], raw[:, ds(at, WP)], ACT.Copy).then_inc(whi_done, 1)

            act.wait_ge(bias_in, 16 * (1 + 3 * B))
            act.wait_ge(x2_done, B)
            for tb in range(NT):
                for k in range(FC):
                    n = FC * tb + k
                    act.wait_ge(fc_up, n + 1)
                    act.wait_ge(fc_h_ready, n + 1)
                    nc.scalar.activation(stage[:, n % PAIR, :], ps[:, 2 * (n % PAIR), :], ACT.Gelu,
                                         bias=fc1_bias[:, k:k + 1]).then_inc(gelu_done, 1)
                    if k % 2 == 1:
                        act.wait_ge(raw_in[tb], 16)
                        weight_piece(1, tb, k // 2, 0)

            def expert_block(e, slot, tb, split):
                for k in range(FC):
                    n = e * (NT * FC) + tb * FC + k
                    act.wait_ge(up_done, n + 1)
                    act.wait_ge(mul_done, n + 1)
                    nc.scalar.activation(stage[:, k % PAIR, :], ps[:, 2 * (k % PAIR), :], ACT.Silu) \
                      .then_inc(silu_done, 1)
                    if split and k % 2 == 1:
                        weight_piece(1 - slot, tb, k // 2, 0)

            act.wait_ge(fc_h_ready, PAIR + NT * FC)

            def expert(e, slot, split):
                if split:
                    act.wait_ge(out_ready, (e + 1) * NT)
                    for q in range(NT):
                        act.wait_ge(raw_in[q], (e + 2) * 16)
                with act.Fori(0, NT) as tb:
                    expert_block(e, slot, tb, split)

            with act.Fori(0, EG // 2) as pair:
                expert(pair * 2, 1, True)
                expert(pair * 2 + 1, 0, True)
            expert(EG, 1, False)

        @block.vector
        def _(dve):
            steps = [0]

            def link(ins):
                steps[0] += 1
                ins.then_inc(dve_step, 1)
                dve.wait_ge(dve_step, steps[0])

            def wide(ap, axis, shape):
                return ap.unsqueeze(axis).to_broadcast(shape)

            nc.vector.sem_inc(gelu_done, PAIR)
            nc.vector.sem_inc(fc_h_ready, PAIR)
            nc.vector.sem_inc(mul_done, PAIR)
            nc.vector.sem_inc(down_done, RING)
            nc.vector.sem_inc(out_free, 1)

            dve.wait_ge(scal_in, 16)
            link(nc.vector.tensor_tensor(c0[:, :], sc_in[:, ZX:ZX + B], sc_in[:, ZY:ZY + B], ALU.add))
            link(nc.vector.tensor_scalar(c0[:, :], c0[:, :], -2.0, 1.0, ALU.mult, ALU.add))
            link(nc.vector.tensor_tensor(c0[:, :], c0[:, :], sc_in[:, ZR:ZR + B], ALU.add))
            nc.vector.tensor_scalar(neg_zr[:, :], sc_in[:, ZR:ZR + B], -1.0, None, ALU.mult).then_inc(coef_done, 1)
            link(nc.vector.tensor_scalar(one_less_sg[:, :], sc_in[:, SG:SG + B], -1.0, 1.0, ALU.mult, ALU.add))
            for t in range(NT):
                b = t // NTB
                link(nc.vector.tensor_scalar(gate[:, 0:EG, t], sc_in[:, GP + b * EG:GP + (b + 1) * EG],
                                             one_less_sg[:, b:b + 1], None, ALU.mult))
                link(nc.vector.tensor_copy(gate[:, EG:E, t], sc_in[:, SG + b:SG + b + 1]))
            dve.wait_ge(types_in, 16)
            link(nc.vector.tensor_copy(type_f[:, :], type_i[:, :]))
            for i in range(2):
                link(nc.vector.tensor_scalar(sel[:, i, :], type_f[:, :], float(i), None, ALU.is_equal))
            link(nc.vector.tensor_tensor(sel[:, 2, :], sel[:, 0, :], sel[:, 1, :], ALU.add))
            link(nc.vector.tensor_scalar(sel[:, 2, :], sel[:, 2, :], -1.0, 1.0, ALU.mult, ALU.add))
            dve.wait_ge(consts_done, 1)
            for b in range(B):
                link(nc.vector.tensor_scalar(blend[:, b, :], blend_src[:, 0, :], sel[:, 0, b:b + 1], None, ALU.mult))
                for i in (1, 2):
                    link(nc.vector.scalar_tensor_tensor(blend[:, b, :], blend_src[:, i, :], sel[:, i, b:b + 1],
                                                        blend[:, b, :], ALU.mult, ALU.add))
            dve.wait_ge(w1_in, 48)
            link(nc.vector.tensor_scalar(v_wide[:, :], ones[0:A, :], v_sb[:, 0:1], None, ALU.mult))

            for b in range(B):
                xTb = xT[:, :, b * S:(b + 1) * S]
                dve.wait_ge(poly_done, b + 1)
                link(nc.vector.tensor_tensor(poly[:, b], poly[:, b], x_pad[:, b, :, 1:S + 1], ALU.mult))
                dve.wait_ge(rows_summed, b + 1)
                dve.wait_ge(edges_done, b + 1)
                nc.vector.tensor_tensor(x_dn[:, b], x_pad[:, b, :, 0:S], x_pad[:, b, :, 2:S + 2], ALU.add) \
                  .then_inc(dve_step, 1)
                steps[0] += 1
                link(nc.vector.scalar_tensor_tensor(poly[:, b], x_up[:, b], sc_in[:, ZX + b:ZX + b + 1], poly[:, b],
                                                    ALU.mult, ALU.add))
                nc.vector.scalar_tensor_tensor(xTb, x_dn[:, b], sc_in[:, ZY + b:ZY + b + 1],
                                               poly[:, b], ALU.mult, ALU.add).then_inc(x1_done, 1)

            KL = [P, KC, P]
            KK = [P, KC, KC]
            for b in range(B):
                mask = blend[:, b, 0:P]
                flag = blend[:, b, P:P + KC * KC].rearrange("p (k c) -> p k c", c=KC)
                scores = ps[:, 4 * b:4 * b + 2, :].rearrange("p n (k l) -> p (n k) l", l=P)
                dve.wait_ge(scores_ps, b + 1)
                link(nc.vector.tensor_tensor(probs[:, b], scores, wide(mask, 1, KL), ALU.add))
                nc.vector.tensor_reduce(chunk_max[:, b, :], scores, AX, ALU.max).then_inc(scores_read, 1)
                link(nc.vector.tensor_reduce(inner_max[:, b, :], probs[:, b], AX, ALU.max))
                dve.wait_ge(scores_read, b + 1)
                link(nc.vector.tensor_tensor(flagged[:, b], flag, wide(chunk_max[:, b, :], 1, KK), ALU.add))
                link(nc.vector.tensor_reduce(outer_max[:, b, :], flagged[:, b], AX, ALU.max))
                link(nc.vector.tensor_tensor(row_max[:, b, :], inner_max[:, b, :], outer_max[:, b, :], ALU.max))
                dve.wait_ge(cols_ps, b + 1)
                ex = exp_in[:, b, 0:KC * KC].rearrange("p (c k) -> p c k", k=KC)
                link(nc.vector.tensor_tensor(ex, flag.rearrange("p k c -> p c k"),
                                             wide(ps[:, 4 * b + 2, 0:KC], 2, KK), ALU.add))
                link(nc.vector.tensor_tensor(ex, ex, wide(outer_max[:, b, :], 1, KK), ALU.subtract))
                nc.vector.tensor_tensor(exp_in[:, b, KC * KC:], outer_max[:, b, :], row_max[:, b, :],
                                        ALU.subtract).then_inc(exps_asked, 1)
                nc.vector.tensor_tensor(probs[:, b], probs[:, b], wide(row_max[:, b, :], 2, KL),
                                        ALU.subtract).then_inc(probs_asked, 1)
            for b in range(B):
                dve.wait_ge(probs_done, b + 1)
                link(nc.vector.tensor_reduce(denom[:, b, :], probs[:, b], AX, ALU.add))
                dve.wait_ge(outer_ps, b + 1)
                nc.vector.tensor_tensor(outer_sum[:, b, :], exp_out[:, b, KC * KC:], ps[:, 4 * b + 2, KC:2 * KC],
                                        ALU.mult).then_inc(outer_read, 1)
                dve.wait_ge(outer_read, b + 1)
                link(nc.vector.tensor_tensor(denom[:, b, :], denom[:, b, :], outer_sum[:, b, :], ALU.add))
                link(nc.vector.tensor_tensor(denom[:, b, :], denom[:, b, :], blend[:, b, P + KC * KC:], ALU.mult))
                link(nc.vector.reciprocal(recip[:, b, :], denom[:, b, :]))
                link(nc.vector.tensor_tensor(outer_w[:, b, :], exp_out[:, b, KC * KC:], recip[:, b, :], ALU.mult))
                link(nc.vector.tensor_tensor(outer_diag[:, b], same_chunk[:, :, :], wide(outer_w[:, b, :], 2, KK),
                                             ALU.mult))
                nc.vector.tensor_tensor(probs[:, b], probs[:, b], wide(recip[:, b, :], 2, KL), ALU.mult) \
                  .then_inc(probs_scaled, 1)

            def split_x(at, size):
                for c in range(DC):
                    link(nc.vector.tensor_copy(x_hi[:, c, at:at + size], xT[:, c, at:at + size]))
                    last = nc.vector.tensor_tensor(x_lo[:, c, at:at + size], xT[:, c, at:at + size],
                                                   x_hi[:, c, at:at + size].bitcast(f32), ALU.subtract)
                return last

            for b in range(B):
                for c in range(DC):
                    dve.wait_ge(pooled_ps, DC * b + c + 1)
                    link(nc.vector.tensor_tensor(xT[:, c, b * S:(b + 1) * S], xT[:, c, b * S:(b + 1) * S],
                                                 ps[:, 4 * b + 2 * c:4 * b + 2 * c + 2, :].rearrange("p n t -> p (n t)"),
                                                 ALU.add))
                split_x(b * S, S).then_inc(x2_done, 1)

            def weight_piece(slot, tb, i, done):
                at = tb * WQ + i * WP
                dve.wait_ge(whi_done, done)
                nc.vector.tensor_tensor(w_lo[slot][:, ds(at, WP)], raw[:, ds(at, WP)],
                                        w_hi[slot][:, ds(at, WP)].bitcast(f32), ALU.subtract).then_inc(wlo_done, 1)

            for tb in range(NT):
                b = tb // NTB
                for k in range(FC):
                    n = FC * tb + k
                    dve.wait_ge(gelu_done, PAIR + n + 1)
                    dve.wait_ge(down_done, n + 1)
                    nc.vector.tensor_copy(h_hi[:, k % RING, :], stage[:, k % PAIR, :]).then_inc(hi_done, 1)
                    dve.wait_ge(hi_done, n + 1)
                    nc.vector.tensor_tensor(h_lo[:, k % RING, :], stage[:, k % PAIR, :],
                                            h_hi[:, k % RING, :].bitcast(f32), ALU.subtract).then_inc(fc_h_ready, 1)
                    if k % 2 == 1:
                        weight_piece(1, tb, k // 2, tb * PIECES + k // 2 + 1)
                dve.wait_ge(out_ready, tb + 1)
                for c in range(DC):
                    xs = xT[:, c, tb * TB:(tb + 1) * TB]
                    last = nc.vector.scalar_tensor_tensor(xs, ps[:, OUT + c, :], out_bias[:, b, c:c + 1], xs,
                                                          ALU.add, ALU.add)
                    steps[0] += 1
                    last.then_inc(dve_step if c < DC - 1 else out_free, 1)
                steps[0] -= 1
                dve.wait_ge(dve_step, steps[0])
                dve.wait_ge(out_free, 1 + tb + 1)
                split_x(tb * TB, TB).then_inc(x3_done, 1)

            def expert_block(e, slot, tb, split):
                for k in range(FC):
                    n = e * (NT * FC) + tb * FC + k
                    dve.wait_ge(silu_done, n + 1)
                    nc.vector.scalar_tensor_tensor(hidden[:, k % PAIR, :], stage[:, k % PAIR, :],
                                                   gate[:, ds(e, 1), ds(tb, 1)].rearrange("p e t -> p (e t)"),
                                                   ps[:, 2 * (k % PAIR) + 1, :], ALU.mult, ALU.mult) \
                      .then_inc(mul_done, 1)
                    dve.wait_ge(down_done, NT * FC + n + 1)
                    dve.wait_ge(mul_done, PAIR + n + 1)
                    nc.vector.tensor_copy(h_hi[:, k % RING, :], hidden[:, k % PAIR, :]).then_inc(hi_done, 1)
                    dve.wait_ge(hi_done, NT * FC + n + 1)
                    nc.vector.tensor_tensor(h_lo[:, k % RING, :], hidden[:, k % PAIR, :],
                                            h_hi[:, k % RING, :].bitcast(f32), ALU.subtract).then_inc(h_ready, 1)
                    if split and k % 2 == 1:
                        weight_piece(1 - slot, tb, k // 2,
                                     (e + 1) * (NT * PIECES) + tb * PIECES + k // 2 + 1)
                dve.wait_ge(out_ready, (e + 1) * NT + tb + 1)
                for c in range(DC):
                    xs = xT[:, c, ds(tb * TB, TB)]
                    last = nc.vector.tensor_tensor(xs, xs, ps[:, OUT + c, :], ALU.add)
                last.then_inc(out_free, 1)

            def expert(e, slot, split):
                with dve.Fori(0, NT) as tb:
                    expert_block(e, slot, tb, split)

            with dve.Fori(0, EG // 2) as pair:
                expert(pair * 2, 1, True)
                expert(pair * 2 + 1, 0, True)
            expert(EG, 1, False)

        @block.tensor
        def _(pe):
            def mm(out_ap, lhsT, rhs, first, last):
                return nc.tensor.matmul(out_ap, lhsT, rhs, start=first, stop=last)

            pe.wait_ge(w1_in, 48)
            for b in range(B):
                pe.wait_ge(x1_done, b + 1)
                for h in range(NTB):
                    for c in range(DC):
                        last = mm(ps[0:A, 4 * b + h, :], w1_sb[:, c, :],
                                  xT[:, c, b * S + h * TB:b * S + (h + 1) * TB], c == 0, c == DC - 1)
                last.then_inc(attn_ps, 1)

            def to_tokens(b, r):
                for k in range(KC // 2):
                    for c in range(DC):
                        at = k * D + c * P
                        s0 = b * S + (r * KC // 2 + k) * P
                        last = nc.tensor.transpose(ps[:, 4 * b + 2 + at // TB, at % TB:at % TB + P],
                                                   xT[:, c, s0:s0 + P], ident[:, :])
                last.then_inc(tok_ps, 1)

            pe.wait_ge(consts_done, 1)
            for b in range(B):
                to_tokens(b, 0)
            for b in range(B):
                pe.wait_ge(attn_done, b + 1)
                for h in range(NTB):
                    last = mm(ps[:, 4 * b + h, :], v_wide[:, :], attn[:, b, h * TB:(h + 1) * TB], True, True)
                last.then_inc(scores_ps, 1)
            for b in range(B):
                pe.wait_ge(tok_done, b + 1)
                to_tokens(b, 1)
            for b in range(B):
                pe.wait_ge(tok_done, B + b + 1)
                for k in range(KC):
                    last = mm(ps[:, 4 * b + 2, k:k + 1], attn[:, b, k * P:(k + 1) * P], v_sb[:, 0:1], True, True)
                last.then_inc(cols_ps, 1)
            for b in range(B):
                pe.wait_ge(exps_done, b + 1)
                for c in range(KC):
                    last = mm(ps[:, 4 * b + 2, KC:2 * KC], ones[:, :], exp_out[:, b, c * KC:(c + 1) * KC],
                              c == 0, c == KC - 1)
                last.then_inc(outer_ps, 1)
                for c in range(KC):
                    last = mm(ps[0:KC, 4 * b + 3, 0:D], exp_out[:, b, c * KC:(c + 1) * KC], x_tok[:, b, c, :],
                              c == 0, c == KC - 1)
                last.then_inc(ctx_ps, 1)
            for b in range(B):
                pe.wait_ge(probs_scaled, b + 1)
                for k in range(KC):
                    at = k * P
                    last = nc.tensor.transpose(ps[:, 4 * b + at // TB, at % TB:at % TB + P], probs[:, b, k, :],
                                               ident[:, :])
                last.then_inc(probst_ps, 1)
                pe.wait_ge(ctx_done, b + 1)
                for k in range(KC):
                    at = k * P
                    last = nc.tensor.transpose(ps[0:KC, 4 * b + 2 + at // TB, at % TB:at % TB + P],
                                               outer_diag[:, b, k, :], ident[:, :])
                last.then_inc(outert_ps, 1)
            for b in range(B):
                pe.wait_ge(probst_done, b + 1)
                pe.wait_ge(outert_done, b + 1)
                for c in range(DC):
                    for h in range(NTB):
                        bank = ps[:, 4 * b + 2 * c + h, :]
                        mm(bank, ctx_sb[:, b, c * P:(c + 1) * P], outer_t[:, b, h * TB:(h + 1) * TB], True, False)
                        for i in range(TB // P):
                            k = h * (TB // P) + i
                            last = mm(bank[:, i * P:(i + 1) * P], x_tok[:, b, k, c * P:(c + 1) * P],
                                      probs_t[:, b, k, :], False, i == TB // P - 1)
                    last.then_inc(pooled_ps, 1)

            def split_mm(out_ap, parts, first, last):
                (wh, wl), (xh, xl) = parts
                mm(out_ap, wh, xh, first, False)
                mm(out_ap, wh, xl, False, False)
                return mm(out_ap, wl, xh, False, last)

            def up(tile_at, bank, k, tokens):
                for c in range(DC):
                    at = tile_at[1] + c * F + k * P
                    hi, lo = w_hi[tile_at[0]], w_lo[tile_at[0]]
                    last = split_mm(ps[:, bank, :], ((hi[:, at:at + P], lo[:, at:at + P]),
                                                     (x_hi[:, c, tokens], x_lo[:, c, tokens])), c == 0, c == DC - 1)
                return last

            def down(weights, k):
                for c in range(DC):
                    wh, wl = weights(c, k)
                    last = split_mm(ps[:, OUT + c, :], ((wh, wl), (h_hi[:, k % RING, :], h_lo[:, k % RING, :])),
                                    k == 0, k == FC - 1)
                return last

            ORDER = [("up", 0), ("up", 1)]
            for k in range(FC - 3):
                ORDER += [("up", k + 2), ("down", k)]
            ORDER[-1:] = []
            ORDER += [("up", FC - 1)] + [("down", k) for k in range(FC - 4, FC)]

            pe.wait_ge(fc_split, 1)
            for tb in range(NT):
                b = tb // NTB
                pe.wait_ge(x2_done, b + 1)
                for kind, k in ORDER:
                    n = FC * tb + k
                    if kind == "up":
                        pe.wait_ge(gelu_done, n + 1)
                        up((0, 0), 2 * (k % PAIR), k, ds(tb * TB, TB)).then_inc(fc_up, 1)
                    else:
                        if k == 0:
                            pe.wait_ge(x2_done, B)
                            pe.wait_ge(out_free, tb + 1)
                        pe.wait_ge(fc_h_ready, PAIR + n + 1)
                        last = down(lambda c, k: (fc2_cols(w_hi[0], b, c)[:, k, :], fc2_cols(w_lo[0], b, c)[:, k, :]), k)
                        last.then_inc(down_done, 1)
                        if k == FC - 1:
                            pe.wait_ge(down_done, RING + n + 1)
                            pe.sem_inc(out_ready, 1)

            def expert_block(e, slot, tb):
                def weights(c, k):
                    at = 2 * UP + k * D + c * P
                    return w_hi[slot][:, at:at + P], w_lo[slot][:, at:at + P]

                for kind, k in ORDER:
                    n = e * (NT * FC) + tb * FC + k
                    if kind == "up":
                        pe.wait_ge(mul_done, n + 1)
                        up((slot, 0), 2 * (k % PAIR), k, ds(tb * TB, TB))
                        up((slot, UP), 2 * (k % PAIR) + 1, k, ds(tb * TB, TB)).then_inc(up_done, 1)
                    else:
                        if k == 0:
                            pe.wait_ge(out_free, (e + 1) * NT + tb + 1)
                        pe.wait_ge(h_ready, n + 1)
                        down(weights, k).then_inc(down_done, 1)
                        if k == FC - 1:
                            pe.wait_ge(down_done, RING + NT * FC + n + 1)
                            pe.sem_inc(out_ready, 1)

            pe.wait_ge(gelu_done, PAIR + NT * FC)
            pe.wait_ge(x3_done, NT)

            def expert(e, slot):
                with pe.Fori(0, NT) as tb:
                    pe.wait_ge(wlo_done, (e + 1) * (NT * PIECES))
                    expert_block(e, slot, tb)

            with pe.Fori(0, EG // 2) as pair:
                expert(pair * 2, 1)
                expert(pair * 2 + 1, 0)
            expert(EG, 1)


def kernel(x, condB_zX, condB_zY, condB_zR, itok_B_0_2, itok_B_0_15, fside_Bx8_0, condB_sharedgateprob,
           L1_cond_W1, L1_cond_b1, L1_cond_v, L2_cond_fc1_w, L2_cond_fc1_b, L2_cond_fc2_w, L2_cond_fc2_b,
           L2_cond_experts_w, L2_cond_experts_b, L3_cond_Wg, L3_cond_Wu, L3_cond_Wd, L3_cond_Sg, L3_cond_Su,
           L3_cond_Sd):
    import numpy as np
    import concourse.bacc as bacc
    from concourse.bass_utils import run_bass_kernel_spmd

    P = 128

    def rows_of(w):
        w = np.asarray(w)
        return np.moveaxis(w.reshape(*w.shape[:-2], w.shape[-2] // P, P, w.shape[-1]), -3, -2)

    def flat(w):
        return w.reshape(*w.shape[:-2], -1)

    x = np.asarray(x)
    D = x.shape[2]
    reflected = [1, *range(D), D - 2]
    moe = [flat(rows_of(np.concatenate([routed, np.asarray(shared)[None]])))
           for routed, shared in ((L3_cond_Wg, L3_cond_Sg), (L3_cond_Wu, L3_cond_Su), (L3_cond_Wd, L3_cond_Sd))]
    arrays = {
        "x_rows": x.transpose(2, 0, 1)[reflected],
        "scalars": np.concatenate([np.asarray(a).ravel() for a in
                                   (condB_zX, condB_zY, condB_zR, condB_sharedgateprob, fside_Bx8_0)]),
        "types": np.asarray(itok_B_0_2),
        "expert_ids": np.asarray(itok_B_0_15),
        "w1": np.asarray(L1_cond_W1),
        "b1": np.asarray(L1_cond_b1),
        "v": np.asarray(L1_cond_v),
        "fc1_w": rows_of(np.asarray(L2_cond_fc1_w).T),
        "fc1_b": np.asarray(L2_cond_fc1_b).reshape(-1, P).T,
        "fc2_w": rows_of(np.asarray(L2_cond_fc2_w).T),
        "fc2_b": np.asarray(L2_cond_fc2_b),
        "experts_w": rows_of(np.asarray(L2_cond_experts_w).transpose(0, 2, 1)),
        "experts_b": np.asarray(L2_cond_experts_b),
        "moe_w": np.concatenate(moe, axis=-1),
    }
    nc = bacc.Bacc("TRN2", target_bir_lowering=False, num_devices=1)
    args, given = [], {}
    for name, a in arrays.items():
        given[f"in_{name}"] = np.ascontiguousarray(a)
        args.append(nc.dram_tensor(f"in_{name}", a.shape, mybir.dt.from_np(a.dtype), kind="ExternalInput").ap())
    B, S, _ = x.shape
    args.append(nc.dram_tensor("out_x", (D, B * S), mybir.dt.float32, kind="ExternalOutput").ap())
    stencil_attention_experts(nc, *args)
    r = run_bass_kernel_spmd(nc, [given], core_ids=[0])
    return np.ascontiguousarray(r.results[0]["out_x"].reshape(D, B, S).transpose(1, 2, 0))
```

```python
import concourse.bass as bass
from concourse import mybir
from contextlib import ExitStack


def stencil_attention_experts(nc, x_rows, scalars, types, expert_ids, w1, b1, v, fc1_w, fc1_b, fc2_w, fc2_b,
                              experts_w, experts_b, moe_w, out):
    f32 = mybir.dt.float32
    f32r = mybir.dt.float32r
    i32 = mybir.dt.int32
    ALU = mybir.AluOpType
    ACT = mybir.ActivationFunctionType
    AX = mybir.AxisListType.X

    P = 128
    B, S = x_rows.shape[1:]
    D = x_rows.shape[0] - 2
    DC = D // P
    T = B * S
    TB = 512
    NT = T // TB
    NTB = S // TB
    A = w1.shape[1]
    F = fc1_b.shape[0] * fc1_b.shape[1]
    FC = F // P
    KC = S // P
    E = moe_w.shape[0]
    EG = E - 1
    WE = moe_w.shape[2]
    WQ = WE // NT
    PIECES = FC // 2
    WP = WQ // PIECES
    UP = DC * F
    SHARED = fc2_w.shape[2]
    NEG = -1e30
    PAIR = 2
    RING = 4
    ds = bass.ds
    WARM = [24, 2, 2, 8, 5]

    with ExitStack() as ctx:
        def sb(name, shape, dt=f32):
            return ctx.enter_context(nc.sbuf_tensor(name, shape, dt))

        def sem(name):
            return ctx.enter_context(nc.semaphore(name))

        xT = sb("xT", [P, DC, T])
        x_hi = sb("x_hi", [P, DC, T], f32r)
        raw = sb("raw", [P, WE])
        w_hi = [sb("w_hi0", [P, WE], f32r)]
        w_lo = [sb("w_lo0", [P, WE], f32r)]
        ident = sb("ident", [P, P])
        ones = sb("ones", [P, P])
        NB = P + KC * KC + KC
        blend_src = sb("blend_src", [P, 3, NB])
        blend = sb("blend", [P, B, NB])
        same_chunk = sb("same_chunk", [P, KC, KC])
        sc_in = sb("sc_in", [P, scalars.shape[0]])
        type_i = sb("type_i", [P, B], i32)
        type_f = sb("type_f", [P, B])
        sel = sb("sel", [P, 3, B])
        ids = sb("ids", [1, B], i32)
        c0 = sb("c0", [P, B])
        neg_zr = sb("neg_zr", [P, B])
        one_less_sg = sb("one_less_sg", [P, B])
        gate = sb("gate", [P, E, NT])
        w1_sb = sb("w1_sb", [P, DC, A])
        b1_sb = sb("b1_sb", [A, 1])
        v_sb = sb("v_sb", [A, 1])
        v_wide = sb("v_wide", [A, P])
        table_probe = sb("table_probe", [A, 1])
        fc1_bias = sb("fc1_bias", [P, FC])
        out_bias = sb("out_bias", [P, B, DC])
        inner_max = sb("inner_max", [P, B, KC])
        chunk_max = sb("chunk_max", [P, B, KC])
        flagged = sb("flagged", [P, B, KC, KC])
        outer_max = sb("outer_max", [P, B, KC])
        row_max = sb("row_max", [P, B, KC])
        exp_in = sb("exp_in", [P, B, KC * KC + KC])
        exp_out = sb("exp_out", [P, B, KC * KC + KC])
        denom = sb("denom", [P, B, KC])
        outer_sum = sb("outer_sum", [P, B, KC])
        recip = sb("recip", [P, B, KC])
        outer_w = sb("outer_w", [P, B, KC])
        outer_diag = sb("outer_diag", [P, B, KC, KC])
        ctx_sb = sb("ctx_sb", [KC, B, D])


        with ExitStack() as early:
            def eb(name, shape, dt=f32):
                return early.enter_context(nc.sbuf_tensor(name, shape, dt))
            nb_all = eb("nb_all", [P, DC, T])
            x_up = eb("x_up", [P, B, DC, S])
            x_dn = eb("x_dn", [P, B, DC, S])
            poly = eb("poly", [P, B, DC, S])
        x_nb = nb_all[:, :, T - S:T]
        x_tok = x_up[:, :, :, :].rearrange("p b c (h s) -> p b (c h) s", s=D)
        attn = x_dn[0:A, :, 0, :]
        probs = x_dn[:, :, 1, :].rearrange("p b (k l) -> p b k l", l=P)
        probs_t = poly[:, :, 0, :].rearrange("p b (k l) -> p b k l", l=P)
        outer_t = poly[0:KC, :, 1, :]
        x_lo = sb("x_lo", [P, DC, T], f32r)
        w_hi.append(sb("w_hi1", [P, WE], f32r))
        w_lo.append(sb("w_lo1", [P, WE], f32r))
        stage = sb("stage", [P, PAIR, TB])
        hidden = sb("hidden", [P, PAIR, TB])
        h_hi = sb("h_hi", [P, RING, TB], f32r)
        h_lo = sb("h_lo", [P, RING, TB], f32r)

        ps = ctx.enter_context(nc.psum_tensor("ps", [P, 8, TB], f32))
        FC_OUT = 2
        OUT = 4
        PAIR_BANK = [0, 6]

        consts_done = sem("consts_done")
        scal_in = sem("scal_in")
        types_in = sem("types_in")
        ids_in = sem("ids_in")
        w1_in = sem("w1_in")
        bias_in = sem("bias_in")
        x_in = [sem(f"x_in{b}") for b in range(B)]
        rows_in = [[sem(f"rows_in{b}_{h}") for h in range(NTB)] for b in range(B)]
        fc1_in = sem("fc1_in")
        fc_in = sem("fc_in")
        raw_in = [sem(f"raw_in{q}") for q in range(NT)]
        dve_step = sem("dve_step")
        coef_done = sem("coef_done")
        pool_step = sem("pool_step")
        rows_summed = sem("rows_summed")
        poly_done = sem("poly_done")
        v_done = sem("v_done")
        x1_done = sem("x1_done")
        attn_ps = sem("attn_ps")
        attn_done = sem("attn_done")
        scores_ps = sem("scores_ps")
        cols_ps = sem("cols_ps")
        tok_ps = sem("tok_ps")
        tok_done = sem("tok_done")
        scores_read = sem("scores_read")
        exps_asked = sem("exps_asked")
        exps_done = sem("exps_done")
        probs_asked = sem("probs_asked")
        probs_done = sem("probs_done")
        outer_ps = sem("outer_ps")
        outer_read = sem("outer_read")
        ctx_ps = sem("ctx_ps")
        ctx_done = sem("ctx_done")
        probs_scaled = sem("probs_scaled")
        outer_scaled = sem("outer_scaled")
        probst_ps = sem("probst_ps")
        probst_done = sem("probst_done")
        outert_ps = sem("outert_ps")
        outert_done = sem("outert_done")
        pooled_ps = sem("pooled_ps")
        x2_done = sem("x2_done")
        fc_hi_split = sem("fc_hi_split")
        fc_split = sem("fc_split")
        fc_up = sem("fc_up")
        gelu_done = sem("gelu_done")
        fc_h_ready = sem("fc_h_ready")
        down_done = sem("down_done")
        out_free = sem("out_free")
        x2_summed = sem("x2_summed")
        x2_hi_done = sem("x2_hi_done")
        fc_summed = sem("fc_summed")
        x3_hi_done = sem("x3_hi_done")
        x3_done = sem("x3_done")
        fc_hi_done = sem("fc_hi_done")
        hi_done = sem("hi_done")
        up_done = sem("up_done")
        silu_done = sem("silu_done")
        mul_done = sem("mul_done")
        h_ready = sem("h_ready")
        whi_done = sem("whi_done")
        wlo_done = sem("wlo_done")
        stored = sem("stored")

        ZX, ZY, ZR, SG, GP = 0, B, 2 * B, 3 * B, 4 * B
        CUTS = [(0, TB + 8), (TB + 8, S)]
        block = ctx.enter_context(nc.Block())

        FC2 = [UP] * B
        FC2B = [UP + FC * P * (1 + b) for b in range(B)]
        FCW = UP + FC * P * (1 + B)
        FCP = FC * P

        def fc2_cols(tile, b, c):
            at = FC2[b] if c == 0 else FC2B[b]
            return tile[:, at:at + FC * P].rearrange("p (k m) -> p k m", m=P)

        @block.sync
        def _(sp):
            def x_load(b):
                sp.dma_start(xT[:, :, b * S:(b + 1) * S],
                             x_rows[1:1 + D, b, :].rearrange("(c p) s -> p c s", p=P)).then_inc(x_in[b], 16)

            def rows_load(b, h):
                s0, s1 = CUTS[h]
                for tile, shift in ((x_up, 2), (x_dn, 0)):
                    sp.dma_start(tile[:, b, :, s0:s1],
                                 x_rows[shift:shift + D, b, s0:s1].rearrange("(c p) s -> p c s", p=P)) \
                      .then_inc(rows_in[b][h], 16)

            x_load(0)
            rows_load(0, 0)
            rows_load(0, 1)
            sp.dma_start(w1_sb[:, :, :], w1.rearrange("(c p) a -> p c a", p=P)).then_inc(w1_in, 16)
            sp.dma_start(b1_sb[:, :], b1.unsqueeze(1)).then_inc(w1_in, 16)
            sp.dma_start(v_sb[:, :], v.unsqueeze(1)).then_inc(w1_in, 16)
            sp.dma_start(raw[:, 0:UP].rearrange("p (c f) -> p c f", c=DC), fc1_w).then_inc(fc1_in, 16)
            sp.dma_start(fc2_cols(raw, 0, 0), fc2_w[:, :, 0:P]).then_inc(fc_in, 16)
            sp.wait_ge(ids_in, 16)
            for b in range(B):
                sp.dma_start(fc2_cols(raw, b, 1)[:, :, 0:SHARED - P], fc2_w[:, :, P:SHARED]).then_inc(fc_in, 16)
                eid = sp.value_load(ids[0:1, b:b + 1], min_val=0, max_val=experts_w.shape[0] - 1)
                sp.dma_start(fc2_cols(raw, b, 1)[:, :, SHARED - P:P],
                             experts_w[ds(eid, 1), :, :, :].rearrange("e p k m -> (e p) k m")).then_inc(fc_in, 16)
                sp.dma_start(out_bias[SHARED - P:P, b, 1:2],
                             experts_b[ds(eid, 1), :].rearrange("e m -> m e")).then_inc(bias_in, 16)
            x_load(1)
            rows_load(1, 0)
            rows_load(1, 1)
            sp.wait_ge(fc_split, FCW // FCP)
            for q in range(NT):
                sp.dma_start(raw[:, q * WQ:(q + 1) * WQ], moe_w[0, :, q * WQ:(q + 1) * WQ]).then_inc(raw_in[q], 16)
            with sp.Fori(1, E) as e:
                for q in range(NT):
                    sp.wait_ge(wlo_done, (e - 1) * (NT * PIECES) + (q + 1) * PIECES)
                    sp.dma_start(raw[:, q * WQ:(q + 1) * WQ],
                                 moe_w[ds(e, 1), :, q * WQ:(q + 1) * WQ].rearrange("e p w -> (e p) w")) \
                      .then_inc(raw_in[q], 16)
            for t in range(NT):
                sp.wait_ge(out_free, 1 + (E - 1) * NT + t + 1)
                sp.dma_start(out.rearrange("(c p) t -> p c t", p=P)[:, :, t * TB:(t + 1) * TB],
                             xT[:, :, t * TB:(t + 1) * TB]).then_inc(stored, 16)
            sp.wait_ge(stored, 16 * NT)

        @block.gpsimd
        def _(pool):
            nc.gpsimd.memset(ident[:, :], 0.0).then_inc(pool_step, 1)
            nc.gpsimd.memset(ones[:, :], 1.0).then_inc(pool_step, 1)
            nc.gpsimd.memset(same_chunk[:, :, :], 0.0).then_inc(pool_step, 1)
            nc.gpsimd.memset(blend_src[:, :, :], 0.0).then_inc(pool_step, 1)
            pool.wait_ge(pool_step, 4)
            masks = [blend_src[:, i, 0:P] for i in range(3)]
            flags = [blend_src[:, i, P:P + KC * KC].rearrange("p (k c) -> p k c", c=KC) for i in range(3)]
            counts = [blend_src[:, i, P + KC * KC:NB] for i in range(3)]

            def fill_where(tile, compare, fill, pattern, row):
                return nc.gpsimd.affine_select(out=tile, in_=tile, compare_op=compare, fill=fill, base=0,
                                               pattern=pattern, channel_multiplier=row)

            fill_where(ident[:, :], ALU.not_equal, 1.0, [[-1, P]], 1)
            fill_where(masks[0], ALU.is_ge, NEG, [[-1, P]], 1)
            fill_where(masks[1], ALU.is_ge, NEG, [[1, P]], -1)
            fill_where(masks[2], ALU.not_equal, NEG, [[-1, P]], 1)
            fill_where(flags[0], ALU.is_gt, NEG, [[1, KC], [-1, KC]], 0)
            fill_where(flags[1], ALU.is_gt, NEG, [[-1, KC], [1, KC]], 0)
            fill_where(flags[2], ALU.not_equal, NEG, [[1, KC], [-1, KC]], 0)
            fill_where(same_chunk[:, :, :], ALU.not_equal, 1.0, [[1, KC], [-1, KC]], 0)
            nc.gpsimd.iota(counts[0], [[P, KC]], base=1, channel_multiplier=1, allow_small_or_imprecise_dtypes=True)
            nc.gpsimd.iota(counts[1], [[-P, KC]], base=S, channel_multiplier=-1, allow_small_or_imprecise_dtypes=True)
            nc.gpsimd.memset(counts[2], float(S - 1)).then_inc(consts_done, 1)

            def rows_sum(b, h):
                s0, s1 = CUTS[h]
                pool.wait_ge(rows_in[b][h], 32)
                nc.gpsimd.tensor_tensor(x_up[:, b, :, s0:s1], x_up[:, b, :, s0:s1], x_dn[:, b, :, s0:s1],
                                        ALU.add).then_inc(rows_summed, 1)

            rows_sum(0, 0)
            rows_sum(0, 1)
            for i in range(FCW // FCP):
                pool.wait_ge(fc_hi_split, i + 1)
                at = i * FCP
                nc.gpsimd.tensor_tensor(w_lo[0][:, at:at + FCP], raw[:, at:at + FCP],
                                        w_hi[0][:, at:at + FCP].bitcast(f32), ALU.subtract).then_inc(fc_split, 1)
            rows_sum(1, 0)
            rows_sum(1, 1)

        @block.scalar
        def _(act):
            act.dma_start(sc_in[:, :], scalars.partition_broadcast(P)).then_inc(scal_in, 16)
            act.dma_start(type_i[:, :], types.partition_broadcast(P)).then_inc(types_in, 16)
            act.dma_start(ids[:, :], expert_ids.unsqueeze(0)).then_inc(ids_in, 16)

            def stencil_poly(b, h):
                s0, s1 = CUTS[h]
                act.wait_ge(x_in[b], 16)
                nc.scalar.activation(poly[:, b, :, s0:s1], xT[:, :, b * S + s0:b * S + s1], ACT.Identity,
                                     bias=c0[:, b:b + 1], scale=neg_zr[:, b:b + 1]).then_inc(poly_done, 1)

            def score_layer(b, h):
                act.wait_ge(attn_ps, b * NTB + h + 1)
                nc.scalar.activation(attn[:, b, h * TB:(h + 1) * TB], ps[0:A, 4 * b + h, :], ACT.Tanh,
                                     bias=b1_sb[:, 0:1]).then_inc(attn_done, 1)

            def tokens_out(b, r):
                act.wait_ge(tok_ps, 2 * b + r + 1)
                nc.scalar.activation(x_tok[:, b, r * KC // 2:(r + 1) * KC // 2, :].rearrange("p k d -> p (k d)"),
                                     ps[:, 4 * b + 2:4 * b + 4, :].rearrange("p n t -> p (n t)"),
                                     ACT.Copy).then_inc(tok_done, 1)

            def outer_exps(b):
                act.wait_ge(exps_asked, b + 1)
                nc.scalar.activation(exp_out[:, b, :], exp_in[:, b, :], ACT.Exp).then_inc(exps_done, 1)

            def inner_exps(b):
                act.wait_ge(probs_asked, b + 1)
                nc.scalar.activation(probs[:, b], probs[:, b], ACT.Exp).then_inc(probs_done, 1)

            def context_out(b):
                act.wait_ge(ctx_ps, b + 1)
                nc.scalar.activation(ctx_sb[:, b, :], ps[0:KC, 4 * b + 3, 0:D], ACT.Copy).then_inc(ctx_done, 1)

            def transposed_out(b):
                act.wait_ge(probst_ps, b + 1)
                nc.scalar.activation(probs_t[:, b].rearrange("p k l -> p (k l)"),
                                     ps[:, 4 * b:4 * b + 2, :].rearrange("p n t -> p (n t)"),
                                     ACT.Copy).then_inc(probst_done, 1)
                act.wait_ge(outert_ps, b + 1)
                nc.scalar.activation(outer_t[:, b, :], ps[0:KC, 4 * b + 2:4 * b + 4, :].rearrange("p n t -> p (n t)"),
                                     ACT.Copy).then_inc(outert_done, 1)

            def fc_weights(first, last):
                for i in range(first, last):
                    nc.scalar.activation(w_hi[0][:, i * FCP:(i + 1) * FCP], raw[:, i * FCP:(i + 1) * FCP],
                                         ACT.Copy).then_inc(fc_hi_split, 1)

            def x_high(tb, summed, done):
                for c in range(DC):
                    act.wait_ge(summed, DC * tb + c + 1)
                    nc.scalar.activation(x_hi[:, c, tb * TB:(tb + 1) * TB], xT[:, c, tb * TB:(tb + 1) * TB],
                                         ACT.Copy).then_inc(done, 1)

            act.wait_ge(coef_done, 1)
            stencil_poly(0, 0)
            stencil_poly(0, 1)
            act.dma_start(fc1_bias[:, :], fc1_b).then_inc(bias_in, 16)
            for b in range(B):
                act.dma_start(out_bias[:, b, 0:1], fc2_b[0:P].unsqueeze(1)).then_inc(bias_in, 16)
                act.dma_start(out_bias[0:SHARED - P, b, 1:2], fc2_b[P:SHARED].unsqueeze(1)).then_inc(bias_in, 16)
            act.wait_ge(w1_in, 48)
            score_layer(0, 0)
            score_layer(0, 1)
            tokens_out(0, 0)
            act.wait_ge(fc1_in, 16)
            fc_weights(0, 1)
            tokens_out(0, 1)
            fc_weights(1, 2)
            act.wait_ge(fc_in, 16 * (1 + 2 * B))
            fc_weights(2, FCW // FCP)
            outer_exps(0)
            inner_exps(0)
            stencil_poly(1, 0)
            stencil_poly(1, 1)
            context_out(0)
            transposed_out(0)
            nc.scalar.activation(table_probe[:, :], b1_sb[:, :], ACT.Gelu)
            x_high(0, x2_summed, x2_hi_done)
            x_high(1, x2_summed, x2_hi_done)

            between = {(0, 5): [lambda: score_layer(1, 0)],
                       (0, 6): [lambda: score_layer(1, 1)],
                       (0, 7): [lambda: tokens_out(1, 0)],
                       (1, 0): [lambda: tokens_out(1, 1)],
                       (1, 2): [lambda: x_high(0, fc_summed, x3_hi_done)],
                       (1, 3): [lambda: outer_exps(1), lambda: inner_exps(1)],
                       (1, 4): [lambda: context_out(1)],
                       (1, 7): [lambda: transposed_out(1), lambda: x_high(2, x2_summed, x2_hi_done)],
                       (2, 1): [lambda: x_high(3, x2_summed, x2_hi_done)],
                       (2, 3): [lambda: x_high(1, fc_summed, x3_hi_done)],
                       (3, 1): [lambda: x_high(2, fc_summed, x3_hi_done)]}

            def weight_piece(slot, tb, i, n):
                at = tb * WQ + i * WP
                nc.scalar.activation(w_hi[slot][:, ds(at, WP)], raw[:, ds(at, WP)], ACT.Copy).then_inc(whi_done, 1)

            act.wait_ge(bias_in, 16 * (1 + 3 * B))
            for tb in range(NT):
                for k in range(FC):
                    n = FC * tb + k
                    act.wait_ge(fc_up, n + 1)
                    act.wait_ge(fc_h_ready, n + 1)
                    nc.scalar.activation(stage[:, n % PAIR, :], ps[:, n % PAIR, :], ACT.Gelu,
                                         bias=fc1_bias[:, k:k + 1]).then_inc(gelu_done, 1)
                    act.wait_ge(down_done, n + 1)
                    act.wait_ge(gelu_done, PAIR + n + 1)
                    nc.scalar.activation(h_hi[:, k % RING, :], stage[:, n % PAIR, :], ACT.Copy).then_inc(fc_hi_done, 1)
                    for stage_of_1 in between.get((tb, k), []):
                        stage_of_1()
                    if tb >= NTB:
                        at = (tb - NTB) * FC + k
                        if at == 0:
                            act.wait_ge(pooled_ps, NT)
                        act.wait_ge(raw_in[at // PIECES], 16)
                        weight_piece(1, at // PIECES, at % PIECES, 0)

            def expert_block(e, slot, tb, split):
                for k in range(FC):
                    n = e * (NT * FC) + tb * FC + k
                    act.wait_ge(up_done, n + 1)
                    act.wait_ge(mul_done, n + 1)
                    nc.scalar.activation(stage[:, k % PAIR, :], ps[:, PAIR_BANK[k % PAIR], :], ACT.Silu) \
                      .then_inc(silu_done, 1)
                    if split and k % 2 == 1:
                        weight_piece(1 - slot, tb, k // 2, 0)

            x_high(NT - 1, fc_summed, x3_hi_done)
            act.wait_ge(fc_h_ready, PAIR + NT * FC)

            def expert(e, slot, split):
                if split:
                    act.wait_ge(down_done, RING + (e + 1) * (NT * FC))
                    for q in range(NT):
                        act.wait_ge(raw_in[q], (e + 2) * 16)
                with act.Fori(0, NT) as tb:
                    expert_block(e, slot, tb, split)

            with act.Fori(0, EG // 2) as pair:
                expert(pair * 2, 1, True)
                expert(pair * 2 + 1, 0, True)
            expert(EG, 1, False)

        @block.vector
        def _(dve):
            steps = [0]

            def link(ins):
                steps[0] += 1
                ins.then_inc(dve_step, 1)
                dve.wait_ge(dve_step, steps[0])

            def wide(ap, axis, shape):
                return ap.unsqueeze(axis).to_broadcast(shape)

            nc.vector.sem_inc(gelu_done, PAIR)
            nc.vector.sem_inc(fc_h_ready, PAIR)
            nc.vector.sem_inc(mul_done, PAIR)
            nc.vector.sem_inc(down_done, RING)
            nc.vector.sem_inc(out_free, 1)

            dve.wait_ge(scal_in, 16)
            link(nc.vector.tensor_tensor(c0[:, :], sc_in[:, ZX:ZX + B], sc_in[:, ZY:ZY + B], ALU.add))
            link(nc.vector.tensor_scalar(c0[:, :], c0[:, :], -2.0, 1.0, ALU.mult, ALU.add))
            link(nc.vector.tensor_tensor(c0[:, :], c0[:, :], sc_in[:, ZR:ZR + B], ALU.add))
            nc.vector.tensor_scalar(neg_zr[:, :], sc_in[:, ZR:ZR + B], -1.0, None, ALU.mult).then_inc(coef_done, 1)
            def gates():
                link(nc.vector.tensor_scalar(one_less_sg[:, :], sc_in[:, SG:SG + B], -1.0, 1.0, ALU.mult, ALU.add))
                for t in range(NT):
                    b = t // NTB
                    link(nc.vector.tensor_scalar(gate[:, 0:EG, t], sc_in[:, GP + b * EG:GP + (b + 1) * EG],
                                                 one_less_sg[:, b:b + 1], None, ALU.mult))
                    link(nc.vector.tensor_copy(gate[:, EG:E, t], sc_in[:, SG + b:SG + b + 1]))

            def masks():
                dve.wait_ge(types_in, 16)
                link(nc.vector.tensor_copy(type_f[:, :], type_i[:, :]))
                for i in range(2):
                    link(nc.vector.tensor_scalar(sel[:, i, :], type_f[:, :], float(i), None, ALU.is_equal))
                link(nc.vector.tensor_tensor(sel[:, 2, :], sel[:, 0, :], sel[:, 1, :], ALU.add))
                link(nc.vector.tensor_scalar(sel[:, 2, :], sel[:, 2, :], -1.0, 1.0, ALU.mult, ALU.add))
                dve.wait_ge(consts_done, 1)
                for b in range(B):
                    link(nc.vector.tensor_scalar(blend[:, b, :], blend_src[:, 0, :], sel[:, 0, b:b + 1], None, ALU.mult))
                    for i in (1, 2):
                        link(nc.vector.scalar_tensor_tensor(blend[:, b, :], blend_src[:, i, :], sel[:, i, b:b + 1],
                                                            blend[:, b, :], ALU.mult, ALU.add))

            def stencil_square(b, h):
                s0, s1 = CUTS[h]
                part = poly[:, b, :, s0:s1]
                dve.wait_ge(poly_done, NTB * b + h + 1)
                link(nc.vector.tensor_tensor(part, part, xT[:, :, b * S + s0:b * S + s1], ALU.mult))

            def stencil_tokens(b, h):
                s0, s1 = CUTS[h]
                xb = xT[:, :, b * S:(b + 1) * S]
                dve.wait_ge(x_in[b], 16)
                if h == 0:
                    nc.vector.tensor_scalar(x_nb[:, :, 0:1], xb[:, :, 1:2], 2.0, None, ALU.mult) \
                      .then_inc(dve_step, 1)
                else:
                    nc.vector.tensor_scalar(x_nb[:, :, S - 1:S], xb[:, :, S - 2:S - 1], 2.0, None, ALU.mult) \
                      .then_inc(dve_step, 1)
                steps[0] += 1
                s0, s1 = max(s0, 1), min(s1, S - 1)
                link(nc.vector.tensor_tensor(x_nb[:, :, s0:s1], xb[:, :, s0 - 1:s1 - 1], xb[:, :, s0 + 1:s1 + 1],
                                             ALU.add))

            def stencil_rows(b, h):
                s0, s1 = CUTS[h]
                part = poly[:, b, :, s0:s1]
                dve.wait_ge(rows_summed, NTB * b + h + 1)
                link(nc.vector.scalar_tensor_tensor(part, x_up[:, b, :, s0:s1], sc_in[:, ZX + b:ZX + b + 1], part,
                                                    ALU.mult, ALU.add))

            def stencil_last(b, h):
                s0, s1 = h * TB, (h + 1) * TB
                nc.vector.scalar_tensor_tensor(xT[:, :, b * S + s0:b * S + s1], x_nb[:, :, s0:s1],
                                               sc_in[:, ZY + b:ZY + b + 1], poly[:, b, :, s0:s1],
                                               ALU.mult, ALU.add).then_inc(x1_done, 1)

            KL = [P, KC, P]
            KK = [P, KC, KC]

            def mask_of(b):
                return blend[:, b, 0:P]

            def flag_of(b):
                return blend[:, b, P:P + KC * KC].rearrange("p (k c) -> p k c", c=KC)

            def scores_of(b):
                return ps[:, 4 * b:4 * b + 2, :].rearrange("p n (k l) -> p (n k) l", l=P)

            def masked_scores(b):
                dve.wait_ge(scores_ps, b + 1)
                link(nc.vector.tensor_tensor(probs[:, b], scores_of(b), wide(mask_of(b), 1, KL), ALU.add))

            def chunk_maxima(b):
                nc.vector.tensor_reduce(chunk_max[:, b, :], scores_of(b), AX, ALU.max).then_inc(scores_read, 1)

            def row_maxima(b):
                link(nc.vector.tensor_reduce(inner_max[:, b, :], probs[:, b], AX, ALU.max))
                dve.wait_ge(scores_read, b + 1)
                link(nc.vector.tensor_tensor(flagged[:, b], flag_of(b), wide(chunk_max[:, b, :], 1, KK), ALU.add))
                link(nc.vector.tensor_reduce(outer_max[:, b, :], flagged[:, b], AX, ALU.max))
                link(nc.vector.tensor_tensor(row_max[:, b, :], inner_max[:, b, :], outer_max[:, b, :], ALU.max))

            def outer_exponents(b):
                dve.wait_ge(cols_ps, b + 1)
                ex = exp_in[:, b, 0:KC * KC].rearrange("p (c k) -> p c k", k=KC)
                link(nc.vector.tensor_tensor(ex, flag_of(b).rearrange("p k c -> p c k"),
                                             wide(ps[:, 4 * b + 2, 0:KC], 2, KK), ALU.add))
                link(nc.vector.tensor_tensor(ex, ex, wide(outer_max[:, b, :], 1, KK), ALU.subtract))
                nc.vector.tensor_tensor(exp_in[:, b, KC * KC:], outer_max[:, b, :], row_max[:, b, :],
                                        ALU.subtract).then_inc(exps_asked, 1)

            def inner_exponents(b):
                nc.vector.tensor_tensor(probs[:, b], probs[:, b], wide(row_max[:, b, :], 2, KL),
                                        ALU.subtract).then_inc(probs_asked, 1)

            def denominators(b):
                dve.wait_ge(probs_done, b + 1)
                link(nc.vector.tensor_reduce(denom[:, b, :], probs[:, b], AX, ALU.add))
                dve.wait_ge(outer_ps, b + 1)
                nc.vector.tensor_tensor(outer_sum[:, b, :], exp_out[:, b, KC * KC:], ps[:, 4 * b + 2, KC:2 * KC],
                                        ALU.mult).then_inc(outer_read, 1)
                dve.wait_ge(outer_read, b + 1)
                link(nc.vector.tensor_tensor(denom[:, b, :], denom[:, b, :], outer_sum[:, b, :], ALU.add))
                link(nc.vector.tensor_tensor(denom[:, b, :], denom[:, b, :], blend[:, b, P + KC * KC:], ALU.mult))
                link(nc.vector.reciprocal(recip[:, b, :], denom[:, b, :]))

            def scaled_weights(b):
                nc.vector.tensor_tensor(probs[:, b], probs[:, b], wide(recip[:, b, :], 2, KL), ALU.mult) \
                  .then_inc(probs_scaled, 1)
                link(nc.vector.tensor_tensor(outer_w[:, b, :], exp_out[:, b, KC * KC:], recip[:, b, :], ALU.mult))
                nc.vector.tensor_tensor(outer_diag[:, b], same_chunk[:, :, :], wide(outer_w[:, b, :], 2, KK),
                                        ALU.mult).then_inc(outer_scaled, 1)

            def x_low(tb, c):
                at = tb * TB
                return nc.vector.tensor_tensor(x_lo[:, c, at:at + TB], xT[:, c, at:at + TB],
                                               x_hi[:, c, at:at + TB].bitcast(f32), ALU.subtract)

            def pooled_added(tb):
                b, h = tb // NTB, tb % NTB
                dve.wait_ge(pooled_ps, tb + 1)
                for c in range(DC):
                    xs = xT[:, c, tb * TB:(tb + 1) * TB]
                    nc.vector.tensor_tensor(xs, xs, ps[:, 4 * b + 2 * c + h, :], ALU.add).then_inc(x2_summed, 1)

            def x2_low(tb):
                for c in range(DC):
                    dve.wait_ge(x2_hi_done, DC * tb + c + 1)
                    last = x_low(tb, c)
                last.then_inc(x2_done, 1)

            def x3_low(tb):
                for c in range(DC):
                    dve.wait_ge(x3_hi_done, DC * tb + c + 1)
                    last = x_low(tb, c)
                last.then_inc(x3_done, 1)

            stencil_tokens(0, 0)
            stencil_tokens(0, 1)
            stencil_square(0, 0)
            stencil_rows(0, 0)
            stencil_last(0, 0)
            stencil_square(0, 1)
            stencil_rows(0, 1)
            stencil_last(0, 1)
            dve.wait_ge(w1_in, 48)
            nc.vector.tensor_scalar(v_wide[:, :], ones[0:A, :], v_sb[:, 0:1], None, ALU.mult).then_inc(v_done, 1)
            masks()
            masked_scores(0)
            chunk_maxima(0)
            row_maxima(0)
            outer_exponents(0)
            inner_exponents(0)
            denominators(0)
            scaled_weights(0)
            gates()
            stencil_square(1, 0)
            stencil_square(1, 1)
            pooled_added(0)
            x2_low(0)
            pooled_added(1)
            x2_low(1)

            between = {(0, 0): [lambda: stencil_tokens(1, 0)],
                       (0, 1): [lambda: stencil_tokens(1, 1), lambda: stencil_rows(1, 0)],
                       (0, 2): [lambda: stencil_last(1, 0)],
                       (0, 3): [lambda: stencil_rows(1, 1)],
                       (0, 4): [lambda: stencil_last(1, 1)],
                       (1, 0): [lambda: masked_scores(1), lambda: chunk_maxima(1)],
                       (1, 1): [lambda: row_maxima(1)],
                       (1, 2): [lambda: outer_exponents(1), lambda: inner_exponents(1)],
                       (1, 3): [lambda: x3_low(0)],
                       (1, 4): [lambda: denominators(1)],
                       (1, 5): [lambda: scaled_weights(1)],
                       (1, 7): [lambda: pooled_added(2), lambda: x2_low(2)],
                       (2, 1): [lambda: pooled_added(3)],
                       (2, 2): [lambda: x2_low(3)],
                       (2, 4): [lambda: x3_low(1)],
                       (3, 2): [lambda: x3_low(2)]}

            def weight_piece(slot, tb, i, done):
                at = tb * WQ + i * WP
                dve.wait_ge(whi_done, done)
                nc.vector.tensor_tensor(w_lo[slot][:, ds(at, WP)], raw[:, ds(at, WP)],
                                        w_hi[slot][:, ds(at, WP)].bitcast(f32), ALU.subtract).then_inc(wlo_done, 1)

            for tb in range(NT):
                b = tb // NTB
                for k in range(FC):
                    n = FC * tb + k
                    dve.wait_ge(fc_hi_done, n + 1)
                    nc.vector.tensor_tensor(h_lo[:, k % RING, :], stage[:, n % PAIR, :],
                                            h_hi[:, k % RING, :].bitcast(f32), ALU.subtract).then_inc(fc_h_ready, 1)
                    for stage_of_1 in between.get((tb, k), []):
                        stage_of_1()
                    if tb >= NTB:
                        at = (tb - NTB) * FC + k
                        weight_piece(1, at // PIECES, at % PIECES, at + 1)
                dve.wait_ge(down_done, RING + FC * (tb + 1))
                for c in range(DC):
                    xs = xT[:, c, tb * TB:(tb + 1) * TB]
                    nc.vector.scalar_tensor_tensor(xs, ps[:, FC_OUT + c, :], out_bias[:, b, c:c + 1], xs,
                                                   ALU.add, ALU.add).then_inc(fc_summed, 1)
            x3_low(NT - 1)

            def expert_block(e, slot, tb, split):
                for k in range(FC):
                    n = e * (NT * FC) + tb * FC + k
                    dve.wait_ge(silu_done, n + 1)
                    nc.vector.scalar_tensor_tensor(hidden[:, k % PAIR, :], stage[:, k % PAIR, :],
                                                   gate[:, ds(e, 1), ds(tb, 1)].rearrange("p e t -> p (e t)"),
                                                   ps[:, PAIR_BANK[k % PAIR] + 1, :], ALU.mult, ALU.mult) \
                      .then_inc(mul_done, 1)
                    dve.wait_ge(down_done, NT * FC + n + 1)
                    dve.wait_ge(mul_done, PAIR + n + 1)
                    nc.vector.tensor_copy(h_hi[:, k % RING, :], hidden[:, k % PAIR, :]).then_inc(hi_done, 1)
                    dve.wait_ge(hi_done, n + 1)
                    nc.vector.tensor_tensor(h_lo[:, k % RING, :], hidden[:, k % PAIR, :],
                                            h_hi[:, k % RING, :].bitcast(f32), ALU.subtract).then_inc(h_ready, 1)
                    if split and k % 2 == 1:
                        weight_piece(1 - slot, tb, k // 2,
                                     (e + 1) * (NT * PIECES) + tb * PIECES + k // 2 + 1)
                dve.wait_ge(down_done, RING + NT * FC + (e * NT + tb + 1) * FC)
                for c in range(DC):
                    xs = xT[:, c, ds(tb * TB, TB)]
                    last = nc.vector.tensor_tensor(xs, xs, ps[:, OUT + c, :], ALU.add)
                last.then_inc(out_free, 1)

            def expert(e, slot, split):
                with dve.Fori(0, NT) as tb:
                    expert_block(e, slot, tb, split)

            with dve.Fori(0, EG // 2) as pair:
                expert(pair * 2, 1, True)
                expert(pair * 2 + 1, 0, True)
            expert(EG, 1, False)

        @block.tensor
        def _(pe):
            def mm(out_ap, lhsT, rhs, first, last):
                return nc.tensor.matmul(out_ap, lhsT, rhs, start=first, stop=last)

            def score_layer(b, h):
                pe.wait_ge(x1_done, b * NTB + h + 1)
                for c in range(DC):
                    last = mm(ps[0:A, 4 * b + h, :], w1_sb[:, c, :], xT[:, c, b * S + h * TB:b * S + (h + 1) * TB],
                              c == 0, c == DC - 1)
                last.then_inc(attn_ps, 1)

            def to_tokens(b, r):
                if r == 1:
                    pe.wait_ge(tok_done, 2 * b + 1)
                for k in range(KC // 2):
                    for c in range(DC):
                        at = k * D + c * P
                        s0 = b * S + (r * KC // 2 + k) * P
                        last = nc.tensor.transpose(ps[:, 4 * b + 2 + at // TB, at % TB:at % TB + P],
                                                   xT[:, c, s0:s0 + P], ident[:, :])
                last.then_inc(tok_ps, 1)

            def scores(b):
                pe.wait_ge(attn_done, NTB * (b + 1))
                for h in range(NTB):
                    last = mm(ps[:, 4 * b + h, :], v_wide[:, :], attn[:, b, h * TB:(h + 1) * TB], True, True)
                last.then_inc(scores_ps, 1)

            def score_columns(b):
                pe.wait_ge(tok_done, 2 * b + 2)
                for k in range(KC):
                    last = mm(ps[:, 4 * b + 2, k:k + 1], attn[:, b, k * P:(k + 1) * P], v_sb[:, 0:1], True, True)
                last.then_inc(cols_ps, 1)

            def outer_sums(b):
                pe.wait_ge(exps_done, b + 1)
                for c in range(KC):
                    last = mm(ps[:, 4 * b + 2, KC:2 * KC], ones[:, :], exp_out[:, b, c * KC:(c + 1) * KC],
                              c == 0, c == KC - 1)
                last.then_inc(outer_ps, 1)
                for c in range(KC):
                    last = mm(ps[0:KC, 4 * b + 3, 0:D], exp_out[:, b, c * KC:(c + 1) * KC], x_tok[:, b, c, :],
                              c == 0, c == KC - 1)
                last.then_inc(ctx_ps, 1)

            def weights_transposed(b):
                pe.wait_ge(probs_scaled, b + 1)
                for k in range(KC):
                    at = k * P
                    last = nc.tensor.transpose(ps[:, 4 * b + at // TB, at % TB:at % TB + P], probs[:, b, k, :],
                                               ident[:, :])
                last.then_inc(probst_ps, 1)
                pe.wait_ge(outer_scaled, b + 1)
                pe.wait_ge(ctx_done, b + 1)
                for k in range(KC):
                    at = k * P
                    last = nc.tensor.transpose(ps[0:KC, 4 * b + 2 + at // TB, at % TB:at % TB + P],
                                               outer_diag[:, b, k, :], ident[:, :])
                last.then_inc(outert_ps, 1)

            def pooled(b, h):
                pe.wait_ge(probst_done, b + 1)
                pe.wait_ge(outert_done, b + 1)
                for c in range(DC):
                    bank = ps[:, 4 * b + 2 * c + h, :]
                    mm(bank, ctx_sb[:, b, c * P:(c + 1) * P], outer_t[:, b, h * TB:(h + 1) * TB], True, False)
                    for i in range(TB // P):
                        k = h * (TB // P) + i
                        last = mm(bank[:, i * P:(i + 1) * P], x_tok[:, b, k, c * P:(c + 1) * P],
                                  probs_t[:, b, k, :], False, i == TB // P - 1)
                last.then_inc(pooled_ps, 1)

            pe.wait_ge(consts_done, 1)
            def keep_warm(n):
                for _ in range(n):
                    mm(ps[:, 7, 0:P], ident[:, :], ident[:, :], True, True)

            pe.wait_ge(x_in[0], 16)
            keep_warm(WARM[0])
            pe.wait_ge(w1_in, 48)
            score_layer(0, 0)
            to_tokens(0, 0)
            keep_warm(WARM[1])
            score_layer(0, 1)
            pe.wait_ge(v_done, 1)
            keep_warm(WARM[2])
            scores(0)
            to_tokens(0, 1)
            score_columns(0)
            keep_warm(WARM[3])
            outer_sums(0)
            weights_transposed(0)
            keep_warm(WARM[4])
            pooled(0, 0)
            pooled(0, 1)

            between = {(0, 4): [lambda: score_layer(1, 0)],
                       (0, 6): [lambda: score_layer(1, 1)],
                       (0, 7): [lambda: to_tokens(1, 0)],
                       (1, 0): [lambda: scores(1)],
                       (1, 1): [lambda: to_tokens(1, 1)],
                       (1, 2): [lambda: score_columns(1)],
                       (1, 4): [lambda: outer_sums(1)],
                       (1, 7): [lambda: weights_transposed(1)]}

            def split_mm(out_ap, parts, first, last):
                (wh, wl), (xh, xl) = parts
                mm(out_ap, wh, xh, first, False)
                mm(out_ap, wh, xl, False, False)
                return mm(out_ap, wl, xh, False, last)

            def up(tile_at, bank, k, tokens):
                for c in range(DC):
                    at = tile_at[1] + c * F + k * P
                    hi, lo = w_hi[tile_at[0]], w_lo[tile_at[0]]
                    last = split_mm(ps[:, bank, :], ((hi[:, at:at + P], lo[:, at:at + P]),
                                                     (x_hi[:, c, tokens], x_lo[:, c, tokens])), c == 0, c == DC - 1)
                return last

            def down(weights, bank, k):
                for c in range(DC):
                    wh, wl = weights(c, k)
                    last = split_mm(ps[:, bank + c, :], ((wh, wl), (h_hi[:, k % RING, :], h_lo[:, k % RING, :])),
                                    k == 0, k == FC - 1)
                return last

            ORDER = [("up", 0), ("up", 1)]
            for k in range(FC - 3):
                ORDER += [("up", k + 2), ("down", k)]
            ORDER[-1:] = []
            ORDER += [("up", FC - 1)] + [("down", k) for k in range(FC - 4, FC)]

            pe.wait_ge(fc_split, UP // FCP)
            for tb in range(NT):
                b = tb // NTB
                pe.wait_ge(x2_done, tb + 1)
                for kind, k in ORDER:
                    n = FC * tb + k
                    if kind == "up":
                        if n == 1:
                            pe.wait_ge(x2_summed, NT)
                        pe.wait_ge(gelu_done, n + 1)
                        up((0, 0), n % PAIR, k, ds(tb * TB, TB)).then_inc(fc_up, 1)
                        for stage_of_1 in between.get((tb, k), []):
                            stage_of_1()
                    else:
                        if k == 0:
                            pe.wait_ge(fc_split, UP // FCP + 2 + b)
                            if tb > 0:
                                pe.wait_ge(fc_summed, DC * tb)
                        pe.wait_ge(fc_h_ready, PAIR + n + 1)
                        last = down(lambda c, k: (fc2_cols(w_hi[0], b, c)[:, k, :], fc2_cols(w_lo[0], b, c)[:, k, :]),
                                    FC_OUT, k)
                        last.then_inc(down_done, 1)
                        if tb == 1 and k == FC - 2:
                            pooled(1, 0)
                            pooled(1, 1)

            def expert_block(e, slot, tb):
                def weights(c, k):
                    at = 2 * UP + k * D + c * P
                    return w_hi[slot][:, at:at + P], w_lo[slot][:, at:at + P]

                for kind, k in ORDER:
                    n = e * (NT * FC) + tb * FC + k
                    if kind == "up":
                        pe.wait_ge(mul_done, n + 1)
                        up((slot, 0), PAIR_BANK[k % PAIR], k, ds(tb * TB, TB))
                        up((slot, UP), PAIR_BANK[k % PAIR] + 1, k, ds(tb * TB, TB)).then_inc(up_done, 1)
                    else:
                        if k == 0:
                            pe.wait_ge(out_free, e * NT + tb + 1)
                        pe.wait_ge(h_ready, n + 1)
                        down(weights, OUT, k).then_inc(down_done, 1)

            pe.wait_ge(gelu_done, PAIR + NT * FC)

            def expert(e, slot):
                with pe.Fori(0, NT) as tb:
                    pe.wait_ge(wlo_done, (e + 1) * (NT * PIECES))
                    pe.wait_ge(x3_done, tb + 1)
                    expert_block(e, slot, tb)

            with pe.Fori(0, EG // 2) as pair:
                expert(pair * 2, 1)
                expert(pair * 2 + 1, 0)
            expert(EG, 1)


def kernel(x, condB_zX, condB_zY, condB_zR, itok_B_0_2, itok_B_0_15, fside_Bx8_0, condB_sharedgateprob,
           L1_cond_W1, L1_cond_b1, L1_cond_v, L2_cond_fc1_w, L2_cond_fc1_b, L2_cond_fc2_w, L2_cond_fc2_b,
           L2_cond_experts_w, L2_cond_experts_b, L3_cond_Wg, L3_cond_Wu, L3_cond_Wd, L3_cond_Sg, L3_cond_Su,
           L3_cond_Sd):
    import numpy as np
    import concourse.bacc as bacc
    from concourse.bass_utils import run_bass_kernel_spmd

    P = 128

    def rows_of(w):
        w = np.asarray(w)
        return np.moveaxis(w.reshape(*w.shape[:-2], w.shape[-2] // P, P, w.shape[-1]), -3, -2)

    def flat(w):
        return w.reshape(*w.shape[:-2], -1)

    x = np.asarray(x)
    D = x.shape[2]
    reflected = [1, *range(D), D - 2]
    moe = [flat(rows_of(np.concatenate([routed, np.asarray(shared)[None]])))
           for routed, shared in ((L3_cond_Wg, L3_cond_Sg), (L3_cond_Wu, L3_cond_Su), (L3_cond_Wd, L3_cond_Sd))]
    arrays = {
        "x_rows": x.transpose(2, 0, 1)[reflected],
        "scalars": np.concatenate([np.asarray(a).ravel() for a in
                                   (condB_zX, condB_zY, condB_zR, condB_sharedgateprob, fside_Bx8_0)]),
        "types": np.asarray(itok_B_0_2),
        "expert_ids": np.asarray(itok_B_0_15),
        "w1": np.asarray(L1_cond_W1),
        "b1": np.asarray(L1_cond_b1),
        "v": np.asarray(L1_cond_v),
        "fc1_w": rows_of(np.asarray(L2_cond_fc1_w).T),
        "fc1_b": np.asarray(L2_cond_fc1_b).reshape(-1, P).T,
        "fc2_w": rows_of(np.asarray(L2_cond_fc2_w).T),
        "fc2_b": np.asarray(L2_cond_fc2_b),
        "experts_w": rows_of(np.asarray(L2_cond_experts_w).transpose(0, 2, 1)),
        "experts_b": np.asarray(L2_cond_experts_b),
        "moe_w": np.concatenate(moe, axis=-1),
    }
    nc = bacc.Bacc("TRN2", target_bir_lowering=False, num_devices=1)
    args, given = [], {}
    for name, a in arrays.items():
        given[f"in_{name}"] = np.ascontiguousarray(a)
        args.append(nc.dram_tensor(f"in_{name}", a.shape, mybir.dt.from_np(a.dtype), kind="ExternalInput").ap())
    B, S, _ = x.shape
    args.append(nc.dram_tensor("out_x", (D, B * S), mybir.dt.float32, kind="ExternalOutput").ap())
    stencil_attention_experts(nc, *args)
    r = run_bass_kernel_spmd(nc, [given], core_ids=[0])
    return np.ascontiguousarray(r.results[0]["out_x"].reshape(D, B, S).transpose(1, 2, 0))
```

```python
import concourse.bass as bass
from concourse import mybir
from contextlib import ExitStack


def stencil_attention_experts(nc, x_rows, scalars, types, expert_ids, w1, b1, v, fc1_w, fc1_b, fc2_w, fc2_b,
                              experts_w, experts_b, moe_w, out):
    f32 = mybir.dt.float32
    f32r = mybir.dt.float32r
    i32 = mybir.dt.int32
    ALU = mybir.AluOpType
    ACT = mybir.ActivationFunctionType
    AX = mybir.AxisListType.X

    P = 128
    B, S = x_rows.shape[1:]
    D = x_rows.shape[0] - 2
    DC = D // P
    T = B * S
    TB = 512
    NT = T // TB
    NTB = S // TB
    A = w1.shape[1]
    F = fc1_b.shape[0] * fc1_b.shape[1]
    FC = F // P
    KC = S // P
    E = moe_w.shape[0]
    EG = E - 1
    WE = moe_w.shape[2]
    WQ = WE // NT
    PIECES = FC // 2
    WP = WQ // PIECES
    UP = DC * F
    SHARED = fc2_w.shape[2]
    NEG = -1e30
    PAIR = 2
    RING = 4
    GROUP = 32
    STACK = 2 * GROUP + KC
    ds = bass.ds
    WARM = [22, 3]

    with ExitStack() as ctx:
        def sb(name, shape, dt=f32):
            return ctx.enter_context(nc.sbuf_tensor(name, shape, dt))

        def sem(name):
            return ctx.enter_context(nc.semaphore(name))

        xT = sb("xT", [P, DC, T])
        x_hi = sb("x_hi", [P, DC, T], f32r)
        raw = sb("raw", [P, WE])
        w_hi = [sb("w_hi0", [P, WE], f32r)]
        w_lo = [sb("w_lo0", [P, WE], f32r)]
        ident = sb("ident", [P, P])
        ones = sb("ones", [P, P])
        NB = P + KC * KC + KC
        blend_src = sb("blend_src", [P, 3, NB])
        chosen = sb("chosen", [P, 3, NB])
        blend = sb("blend", [P, B, NB])
        own_chunk = sb("own_chunk", [STACK, KC])
        sc_in = sb("sc_in", [P, scalars.shape[0]])
        type_i = sb("type_i", [P, B], i32)
        type_f = sb("type_f", [P, B])
        sel = sb("sel", [P, 3, B])
        ids = sb("ids", [1, B], i32)
        c0 = sb("c0", [P, B])
        neg_zr = sb("neg_zr", [P, B])
        one_less_sg = sb("one_less_sg", [P, B])
        gate = sb("gate", [P, E, NT])
        w1_sb = sb("w1_sb", [P, DC, A])
        b1_sb = sb("b1_sb", [A, 1])
        v_sb = sb("v_sb", [A, 1])
        v_wide = sb("v_wide", [A, P])
        table_probe = sb("table_probe", [A, 1])
        fc1_bias = sb("fc1_bias", [P, FC])
        out_bias = sb("out_bias", [P, B, DC])
        inner_max = sb("inner_max", [P, B, KC])
        chunk_max = sb("chunk_max", [P, B, KC])
        flagged = sb("flagged", [P, B, KC, KC])
        outer_max = sb("outer_max", [P, B, KC])
        row_max = sb("row_max", [P, B, KC])
        exp_in = sb("exp_in", [P, B, KC * KC + KC])
        exp_out = sb("exp_out", [P, B, KC * KC + KC])
        denom = sb("denom", [P, B, KC])
        outer_sum = sb("outer_sum", [P, B, KC])
        recip = sb("recip", [P, B, KC])
        outer_w = sb("outer_w", [P, B, STACK])
        outer_rows = sb("outer_rows", [STACK, B, P], f32r)
        ctx_parts = sb("ctx_parts", [STACK, B, D], f32r)

        with ExitStack() as early:
            def eb(name, shape, dt=f32):
                return early.enter_context(nc.sbuf_tensor(name, shape, dt))
            nb_all = eb("nb_all", [P, DC, T])
            x_up = eb("x_up", [P, B, DC, S])
            x_dn = eb("x_dn", [P, B, DC, S])
            poly = eb("poly", [P, B, DC, S])
        x_nb = nb_all[:, :, T - S:T]
        x_tok = x_up[:, :, :, :].rearrange("p b c (h s) -> p b (c h) s", s=D)
        attn = x_dn[0:A, :, 0, :]
        probs = x_dn[:, :, 1, :].rearrange("p b (k l) -> p b k l", l=P)
        probs_t = poly[:, :, 0, :].rearrange("p b (k l) -> p b k l", l=P)
        x_lo = sb("x_lo", [P, DC, T], f32r)
        w_hi.append(sb("w_hi1", [P, WE], f32r))
        w_lo.append(sb("w_lo1", [P, WE], f32r))
        POLY = 2 * B * DC * S - WE
        outer_t = w_lo[1][0:STACK, POLY:POLY + B * DC * S].rearrange("p (b c s) -> p b c s", b=B, c=DC)[:, :, 1, :]
        stage = sb("stage", [P, PAIR, TB])
        hidden = sb("hidden", [P, PAIR, TB])
        h_hi = sb("h_hi", [P, RING, TB], f32r)
        h_lo = sb("h_lo", [P, RING, TB], f32r)

        ps = ctx.enter_context(nc.psum_tensor("ps", [P, 8, TB], f32))
        FC_OUT = 2
        OUT = 4
        PAIR_BANK = [0, 6]
        TOK_BANK = [[2, 4], [6, 6]]
        COL_BANK = 6
        SUMS = slice(KC, KC + KC * KC)

        consts_done = sem("consts_done")
        scal_in = sem("scal_in")
        types_in = sem("types_in")
        ids_in = sem("ids_in")
        w1_in = sem("w1_in")
        bias_in = sem("bias_in")
        x_in = [[sem(f"x_in{b}_{h}") for h in range(NTB)] for b in range(B)]
        rows_in = [[sem(f"rows_in{b}_{h}") for h in range(NTB)] for b in range(B)]
        fc1_in = sem("fc1_in")
        fc_in = sem("fc_in")
        raw_in = [sem(f"raw_in{q}") for q in range(NT)]
        dve_step = sem("dve_step")
        coef_done = sem("coef_done")
        pool_step = sem("pool_step")
        rows_summed = sem("rows_summed")
        tokens_summed = sem("tokens_summed")
        poly_done = sem("poly_done")
        v_done = sem("v_done")
        masks_done = sem("masks_done")
        x1_done = sem("x1_done")
        attn_ps = sem("attn_ps")
        attn_done = sem("attn_done")
        scores_ps = sem("scores_ps")
        cols_ps = sem("cols_ps")
        tok_ps = sem("tok_ps")
        tok_done = sem("tok_done")
        maxima_done = sem("maxima_done")
        exps_asked = sem("exps_asked")
        exps_done = sem("exps_done")
        probs_asked = sem("probs_asked")
        probs_done = sem("probs_done")
        outer_ps = sem("outer_ps")
        outer_read = sem("outer_read")
        ctx_ps = sem("ctx_ps")
        ctx_hi_done = sem("ctx_hi_done")
        ctx_done = sem("ctx_done")
        probs_scaled = sem("probs_scaled")
        outer_scaled = sem("outer_scaled")
        rows_hi_done = sem("rows_hi_done")
        probst_ps = sem("probst_ps")
        probst_done = sem("probst_done")
        outert_ps = sem("outert_ps")
        outert_done = sem("outert_done")
        pooled_ps = sem("pooled_ps")
        x2_done = sem("x2_done")
        fc_hi_split = sem("fc_hi_split")
        fc_split = sem("fc_split")
        fc_up = sem("fc_up")
        gelu_done = sem("gelu_done")
        fc_h_ready = sem("fc_h_ready")
        down_done = sem("down_done")
        out_free = sem("out_free")
        x2_summed = sem("x2_summed")
        x2_hi_done = sem("x2_hi_done")
        fc_summed = sem("fc_summed")
        x3_hi_done = sem("x3_hi_done")
        x3_done = sem("x3_done")
        fc_hi_done = sem("fc_hi_done")
        hi_done = sem("hi_done")
        up_done = sem("up_done")
        silu_done = sem("silu_done")
        mul_done = sem("mul_done")
        h_ready = sem("h_ready")
        whi_done = sem("whi_done")
        wlo_done = sem("wlo_done")
        stored = sem("stored")

        ZX, ZY, ZR, SG, GP = 0, B, 2 * B, 3 * B, 4 * B
        CUTS = [(0, TB + 8), (TB + 8, S)]
        block = ctx.enter_context(nc.Block())

        FC2 = [UP] * B
        FC2B = [UP + FC * P * (1 + b) for b in range(B)]
        FCW = UP + FC * P * (1 + B)
        FCP = FC * P

        def fc2_cols(tile, b, c):
            at = FC2[b] if c == 0 else FC2B[b]
            return tile[:, at:at + FC * P].rearrange("p (k m) -> p k m", m=P)

        @block.sync
        def _(sp):
            def x_load(b, h):
                s0, s1 = ((0, CUTS[0][1] + 8), (CUTS[0][1] + 8, S))[h]
                sp.dma_start(xT[:, :, b * S + s0:b * S + s1],
                             x_rows[1:1 + D, b, s0:s1].rearrange("(c p) s -> p c s", p=P)).then_inc(x_in[b][h], 16)

            def rows_load(b, h):
                s0, s1 = CUTS[h]
                for tile, shift in ((x_up, 2), (x_dn, 0)):
                    sp.dma_start(tile[:, b, :, s0:s1],
                                 x_rows[shift:shift + D, b, s0:s1].rearrange("(c p) s -> p c s", p=P)) \
                      .then_inc(rows_in[b][h], 16)

            x_load(0, 0)
            rows_load(0, 0)
            x_load(0, 1)
            rows_load(0, 1)
            sp.dma_start(w1_sb[:, :, :], w1.rearrange("(c p) a -> p c a", p=P)).then_inc(w1_in, 16)
            sp.dma_start(b1_sb[:, :], b1.unsqueeze(1)).then_inc(w1_in, 16)
            sp.dma_start(v_sb[:, :], v.unsqueeze(1)).then_inc(w1_in, 16)
            sp.dma_start(raw[:, 0:UP].rearrange("p (c f) -> p c f", c=DC), fc1_w).then_inc(fc1_in, 16)
            sp.dma_start(fc2_cols(raw, 0, 0), fc2_w[:, :, 0:P]).then_inc(fc_in, 16)
            sp.wait_ge(ids_in, 16)
            for b in range(B):
                sp.dma_start(fc2_cols(raw, b, 1)[:, :, 0:SHARED - P], fc2_w[:, :, P:SHARED]).then_inc(fc_in, 16)
                eid = sp.value_load(ids[0:1, b:b + 1], min_val=0, max_val=experts_w.shape[0] - 1)
                sp.dma_start(fc2_cols(raw, b, 1)[:, :, SHARED - P:P],
                             experts_w[ds(eid, 1), :, :, :].rearrange("e p k m -> (e p) k m")).then_inc(fc_in, 16)
                sp.dma_start(out_bias[SHARED - P:P, b, 1:2],
                             experts_b[ds(eid, 1), :].rearrange("e m -> m e")).then_inc(bias_in, 16)
            x_load(1, 0)
            x_load(1, 1)
            rows_load(1, 0)
            rows_load(1, 1)
            sp.wait_ge(fc_split, FCW // FCP)
            for q in range(NT):
                sp.dma_start(raw[:, q * WQ:(q + 1) * WQ], moe_w[0, :, q * WQ:(q + 1) * WQ]).then_inc(raw_in[q], 16)
            with sp.Fori(1, E) as e:
                for q in range(NT):
                    sp.wait_ge(wlo_done, (e - 1) * (NT * PIECES) + (q + 1) * PIECES)
                    sp.dma_start(raw[:, q * WQ:(q + 1) * WQ],
                                 moe_w[ds(e, 1), :, q * WQ:(q + 1) * WQ].rearrange("e p w -> (e p) w")) \
                      .then_inc(raw_in[q], 16)
            for t in range(NT):
                for c in range(DC):
                    sp.wait_ge(out_free, DC * (1 + (E - 1) * NT + t) + c + 1)
                    sp.dma_start(out.rearrange("(c p) t -> p c t", p=P)[:, c, t * TB:(t + 1) * TB],
                                 xT[:, c, t * TB:(t + 1) * TB]).then_inc(stored, 16)
            sp.wait_ge(stored, 16 * NT * DC)

        @block.gpsimd
        def _(pool):
            nc.gpsimd.memset(ident[:, :], 0.0).then_inc(pool_step, 1)
            nc.gpsimd.memset(ones[:, :], 1.0).then_inc(pool_step, 1)
            nc.gpsimd.memset(own_chunk[:, :], 0.0).then_inc(pool_step, 1)
            nc.gpsimd.memset(outer_w[:, :, :], 0.0).then_inc(pool_step, 1)
            nc.gpsimd.memset(ctx_parts[:, :, :].bitcast(f32), 0.0).then_inc(pool_step, 1)
            nc.gpsimd.memset(blend_src[:, :, :], 0.0).then_inc(pool_step, 1)
            pool.wait_ge(pool_step, 6)
            masks = [blend_src[:, i, 0:P] for i in range(3)]
            flags = [blend_src[:, i, P:P + KC * KC].rearrange("p (k c) -> p k c", c=KC) for i in range(3)]
            counts = [blend_src[:, i, P + KC * KC:NB] for i in range(3)]

            def fill_where(tile, compare, fill, pattern, row, base=0):
                return nc.gpsimd.affine_select(out=tile, in_=tile, compare_op=compare, fill=fill, base=base,
                                               pattern=pattern, channel_multiplier=row)

            fill_where(ident[:, :], ALU.not_equal, 1.0, [[-1, P]], 1)
            fill_where(masks[0], ALU.is_ge, NEG, [[-1, P]], 1)
            fill_where(masks[1], ALU.is_ge, NEG, [[1, P]], -1)
            fill_where(masks[2], ALU.not_equal, NEG, [[-1, P]], 1)
            fill_where(flags[0], ALU.is_gt, NEG, [[1, KC], [-1, KC]], 0)
            fill_where(flags[1], ALU.is_gt, NEG, [[-1, KC], [1, KC]], 0)
            fill_where(flags[2], ALU.not_equal, NEG, [[1, KC], [-1, KC]], 0)
            for group in range(3):
                if group > 0:
                    pool.wait_ge(pool_step, 6 + group)
                fill_where(own_chunk[:, :], ALU.not_equal, 1.0, [[-1, KC]], 1, -GROUP * group).then_inc(pool_step, 1)
            nc.gpsimd.iota(counts[0], [[P, KC]], base=1, channel_multiplier=1, allow_small_or_imprecise_dtypes=True)
            nc.gpsimd.iota(counts[1], [[-P, KC]], base=S, channel_multiplier=-1, allow_small_or_imprecise_dtypes=True)
            nc.gpsimd.memset(counts[2], float(S - 1)).then_inc(consts_done, 1)

            def rows_sum(b, h):
                s0, s1 = CUTS[h]
                pool.wait_ge(rows_in[b][h], 32)
                nc.gpsimd.tensor_tensor(x_up[:, b, :, s0:s1], x_up[:, b, :, s0:s1], x_dn[:, b, :, s0:s1],
                                        ALU.add).then_inc(rows_summed, 1)

            def tokens_sum(b, h):
                s0, s1 = CUTS[h]
                xb = xT[:, :, b * S:(b + 1) * S]
                pool.wait_ge(x_in[b][h], 16)
                edge, inner = ((0, 1), (S - 1, S - 2))[h]
                nc.gpsimd.tensor_scalar(x_nb[:, :, edge:edge + 1], xb[:, :, inner:inner + 1], 2.0, None, ALU.mult) \
                  .then_inc(tokens_summed, 1)
                s0, s1 = max(s0, 1), min(s1, S - 1)
                nc.gpsimd.tensor_tensor(x_nb[:, :, s0:s1], xb[:, :, s0 - 1:s1 - 1], xb[:, :, s0 + 1:s1 + 1],
                                        ALU.add).then_inc(tokens_summed, 1)

            pool_steps = [9]

            def link(ins):
                pool_steps[0] += 1
                ins.then_inc(pool_step, 1)
                pool.wait_ge(pool_step, pool_steps[0])

            def chosen_masks(b):
                if b > 0:
                    pool.wait_ge(masks_done, b)
                link(nc.gpsimd.tensor_tensor(chosen[:, :, :], blend_src[:, :, :],
                                             sel[:, :, b].unsqueeze(2).to_broadcast([P, 3, NB]), ALU.mult))

            def blended_masks(b):
                link(nc.gpsimd.tensor_tensor(blend[:, b, :], chosen[:, 0, :], chosen[:, 1, :], ALU.add))
                nc.gpsimd.tensor_tensor(blend[:, b, :], blend[:, b, :], chosen[:, 2, :],
                                        ALU.add).then_inc(masks_done, 1)

            pool.wait_ge(types_in, 16)
            link(nc.gpsimd.tensor_copy(type_f[:, :], type_i[:, :]))
            for i in range(2):
                link(nc.gpsimd.tensor_scalar(sel[:, i, :], type_f[:, :], float(i), None, ALU.is_equal))
            link(nc.gpsimd.tensor_tensor(sel[:, 2, :], sel[:, 0, :], sel[:, 1, :], ALU.add))
            link(nc.gpsimd.tensor_scalar(sel[:, 2, :], sel[:, 2, :], -1.0, 1.0, ALU.mult, ALU.add))
            rows_sum(0, 0)
            pool.wait_ge(consts_done, 1)
            chosen_masks(0)
            rows_sum(0, 1)
            pool.wait_ge(w1_in, 48)
            nc.gpsimd.tensor_tensor(v_wide[:, :], ones[0:A, :], v_sb[:, 0:1].to_broadcast([A, P]),
                                    ALU.mult).then_inc(v_done, 1)
            blended_masks(0)
            chosen_masks(1)
            blended_masks(1)
            for i in range(FCW // FCP):
                if i == FCW // FCP - 1:
                    for h in range(NTB):
                        rows_sum(1, h)
                    for h in range(NTB):
                        tokens_sum(1, h)
                pool.wait_ge(fc_hi_split, i + 1)
                at = i * FCP
                nc.gpsimd.tensor_tensor(w_lo[0][:, at:at + FCP], raw[:, at:at + FCP],
                                        w_hi[0][:, at:at + FCP].bitcast(f32), ALU.subtract).then_inc(fc_split, 1)

        @block.scalar
        def _(act):
            act.dma_start(sc_in[:, :], scalars.partition_broadcast(P)).then_inc(scal_in, 16)
            act.dma_start(type_i[:, :], types.partition_broadcast(P)).then_inc(types_in, 16)
            act.dma_start(ids[:, :], expert_ids.unsqueeze(0)).then_inc(ids_in, 16)

            def stencil_poly(b, h):
                s0, s1 = CUTS[h]
                act.wait_ge(x_in[b][h], 16)
                nc.scalar.activation(poly[:, b, :, s0:s1], xT[:, :, b * S + s0:b * S + s1], ACT.Identity,
                                     bias=c0[:, b:b + 1], scale=neg_zr[:, b:b + 1]).then_inc(poly_done, 1)

            def score_layer(b, h):
                act.wait_ge(attn_ps, b * NTB + h + 1)
                nc.scalar.activation(attn[:, b, h * TB:(h + 1) * TB], ps[0:A, 4 * b + h, :], ACT.Tanh,
                                     bias=b1_sb[:, 0:1]).then_inc(attn_done, 1)

            def tokens_out(b, r):
                act.wait_ge(tok_ps, 2 * b + r + 1)
                act.wait_ge(x1_done, NTB * (b + 1))
                nc.scalar.activation(x_tok[:, b, r * KC // 2:(r + 1) * KC // 2, :].rearrange("p k d -> p (k d)"),
                                     ps[:, TOK_BANK[b][r]:TOK_BANK[b][r] + 2, :].rearrange("p n t -> p (n t)"),
                                     ACT.Copy).then_inc(tok_done, 1)

            def outer_exps(b):
                act.wait_ge(exps_asked, b + 1)
                nc.scalar.activation(exp_out[:, b, :], exp_in[:, b, :], ACT.Exp).then_inc(exps_done, 1)

            def inner_exps(b, h):
                act.wait_ge(probs_asked, NTB * b + h + 1)
                part = probs[:, b, h * KC // NTB:(h + 1) * KC // NTB]
                nc.scalar.activation(part, part, ACT.Exp).then_inc(probs_done, 1)

            def context_out(b):
                act.wait_ge(ctx_ps, b + 1)
                for group in (0, 1):
                    nc.scalar.activation(ctx_parts[GROUP * group:GROUP * group + KC, b, :], ps[0:KC, 4 * b + 3, 0:D],
                                         ACT.Copy).then_inc(ctx_hi_done, 1)

            def transposed_out(b, h):
                act.wait_ge(probst_ps, NTB * b + h + 1)
                nc.scalar.activation(probs_t[:, b, h * KC // NTB:(h + 1) * KC // NTB, :].rearrange("p k l -> p (k l)"),
                                     ps[:, 4 * b + h, :], ACT.Copy).then_inc(probst_done, 1)

            def fc_weights(first, last):
                for i in range(first, last):
                    nc.scalar.activation(w_hi[0][:, i * FCP:(i + 1) * FCP], raw[:, i * FCP:(i + 1) * FCP],
                                         ACT.Copy).then_inc(fc_hi_split, 1)

            def x_high(tb, summed, done):
                for c in range(DC):
                    act.wait_ge(summed, DC * tb + c + 1)
                    nc.scalar.activation(x_hi[:, c, tb * TB:(tb + 1) * TB], xT[:, c, tb * TB:(tb + 1) * TB],
                                         ACT.Copy).then_inc(done, 1)

            act.wait_ge(pool_step, 2)
            nc.scalar.activation(table_probe[:, :], ones[0:A, 0:1], ACT.Tanh)
            act.wait_ge(coef_done, 1)
            stencil_poly(0, 0)
            stencil_poly(0, 1)
            act.dma_start(fc1_bias[:, :], fc1_b).then_inc(bias_in, 16)
            for b in range(B):
                act.dma_start(out_bias[:, b, 0:1], fc2_b[0:P].unsqueeze(1)).then_inc(bias_in, 16)
                act.dma_start(out_bias[0:SHARED - P, b, 1:2], fc2_b[P:SHARED].unsqueeze(1)).then_inc(bias_in, 16)
            act.wait_ge(w1_in, 48)
            score_layer(0, 0)
            score_layer(0, 1)
            act.wait_ge(fc1_in, 16)
            fc_weights(0, 2)
            tokens_out(0, 0)
            outer_exps(0)
            inner_exps(0, 0)
            inner_exps(0, 1)
            tokens_out(0, 1)
            act.wait_ge(fc_in, 16 * (1 + 2 * B))
            fc_weights(2, 4)
            context_out(0)
            transposed_out(0, 0)
            transposed_out(0, 1)
            nc.scalar.activation(table_probe[:, :], b1_sb[:, :], ACT.Gelu)
            stencil_poly(1, 0)
            stencil_poly(1, 1)
            x_high(0, x2_summed, x2_hi_done)
            x_high(1, x2_summed, x2_hi_done)

            between = {(0, 3): [lambda: fc_weights(4, FCW // FCP)],
                       (0, 5): [lambda: score_layer(1, 0)],
                       (0, 7): [lambda: tokens_out(1, 0), lambda: score_layer(1, 1)],
                       (1, 0): [lambda: tokens_out(1, 1)],
                       (1, 2): [lambda: x_high(0, fc_summed, x3_hi_done)],
                       (1, 3): [lambda: outer_exps(1), lambda: inner_exps(1, 0), lambda: inner_exps(1, 1)],
                       (1, 4): [lambda: context_out(1)],
                       (1, 7): [lambda: transposed_out(1, 0), lambda: transposed_out(1, 1),
                                lambda: x_high(2, x2_summed, x2_hi_done)],
                       (2, 1): [lambda: x_high(3, x2_summed, x2_hi_done)],
                       (2, 3): [lambda: x_high(1, fc_summed, x3_hi_done)],
                       (3, 1): [lambda: x_high(2, fc_summed, x3_hi_done)]}

            def weight_piece(slot, tb, i):
                at = tb * WQ + i * WP
                nc.scalar.activation(w_hi[slot][:, ds(at, WP)], raw[:, ds(at, WP)], ACT.Copy).then_inc(whi_done, 1)

            act.wait_ge(bias_in, 16 * (1 + 3 * B))
            for tb in range(NT):
                for k in range(FC):
                    n = FC * tb + k
                    act.wait_ge(fc_up, n + 1)
                    act.wait_ge(fc_h_ready, n + 1)
                    nc.scalar.activation(stage[:, n % PAIR, :], ps[:, n % PAIR, :], ACT.Gelu,
                                         bias=fc1_bias[:, k:k + 1]).then_inc(gelu_done, 1)
                    act.wait_ge(down_done, n + 1)
                    act.wait_ge(gelu_done, PAIR + n + 1)
                    nc.scalar.activation(h_hi[:, k % RING, :], stage[:, n % PAIR, :], ACT.Copy).then_inc(fc_hi_done, 1)
                    for stage_of_1 in between.get((tb, k), []):
                        stage_of_1()
                    if tb >= NTB:
                        at = (tb - NTB) * FC + k
                        if at == 0:
                            act.wait_ge(pooled_ps, NT)
                        act.wait_ge(raw_in[at // PIECES], 16)
                        weight_piece(1, at // PIECES, at % PIECES)

            def expert_block(e, slot, tb, split):
                for k in range(FC):
                    n = e * (NT * FC) + tb * FC + k
                    act.wait_ge(up_done, n + 1)
                    act.wait_ge(mul_done, n + 1)
                    nc.scalar.activation(stage[:, k % PAIR, :], ps[:, PAIR_BANK[k % PAIR], :], ACT.Silu) \
                      .then_inc(silu_done, 1)
                    if split and k % 2 == 1:
                        weight_piece(1 - slot, tb, k // 2)

            x_high(NT - 1, fc_summed, x3_hi_done)
            act.wait_ge(fc_h_ready, PAIR + NT * FC)

            def expert(e, slot, split):
                if split:
                    act.wait_ge(down_done, RING + (e + 1) * (NT * FC))
                    for q in range(NT):
                        act.wait_ge(raw_in[q], (e + 2) * 16)
                with act.Fori(0, NT) as tb:
                    expert_block(e, slot, tb, split)

            with act.Fori(0, EG // 2) as pair:
                expert(pair * 2, 1, True)
                expert(pair * 2 + 1, 0, True)
            expert(EG, 1, False)

        @block.vector
        def _(dve):
            steps = [0]

            def link(ins):
                steps[0] += 1
                ins.then_inc(dve_step, 1)
                dve.wait_ge(dve_step, steps[0])

            def wide(ap, axis, shape):
                return ap.unsqueeze(axis).to_broadcast(shape)

            nc.vector.sem_inc(gelu_done, PAIR)
            nc.vector.sem_inc(fc_h_ready, PAIR)
            nc.vector.sem_inc(mul_done, PAIR)
            nc.vector.sem_inc(down_done, RING)
            nc.vector.sem_inc(out_free, DC)

            dve.wait_ge(scal_in, 16)
            link(nc.vector.tensor_tensor(c0[:, :], sc_in[:, ZX:ZX + B], sc_in[:, ZY:ZY + B], ALU.add))
            link(nc.vector.tensor_scalar(c0[:, :], c0[:, :], -2.0, 1.0, ALU.mult, ALU.add))
            link(nc.vector.tensor_tensor(c0[:, :], c0[:, :], sc_in[:, ZR:ZR + B], ALU.add))
            nc.vector.tensor_scalar(neg_zr[:, :], sc_in[:, ZR:ZR + B], -1.0, None, ALU.mult).then_inc(coef_done, 1)

            def gates():
                link(nc.vector.tensor_scalar(one_less_sg[:, :], sc_in[:, SG:SG + B], -1.0, 1.0, ALU.mult, ALU.add))
                for b in range(B):
                    blocks = slice(b * NTB, (b + 1) * NTB)
                    link(nc.vector.tensor_scalar(gate[:, 0:EG, blocks],
                                                 wide(sc_in[:, GP + b * EG:GP + (b + 1) * EG], 2, [P, EG, NTB]),
                                                 one_less_sg[:, b:b + 1], None, ALU.mult))
                    link(nc.vector.tensor_copy(gate[:, EG, blocks], sc_in[:, SG + b:SG + b + 1].to_broadcast([P, NTB])))

            def stencil_square(b, h):
                s0, s1 = CUTS[h]
                part = poly[:, b, :, s0:s1]
                dve.wait_ge(poly_done, NTB * b + h + 1)
                link(nc.vector.tensor_tensor(part, part, xT[:, :, b * S + s0:b * S + s1], ALU.mult))

            def stencil_tokens(b, h):
                s0, s1 = CUTS[h]
                xb = xT[:, :, b * S:(b + 1) * S]
                dve.wait_ge(x_in[b][h], 16)
                if h == 0:
                    nc.vector.tensor_scalar(x_nb[:, :, 0:1], xb[:, :, 1:2], 2.0, None, ALU.mult) \
                      .then_inc(dve_step, 1)
                else:
                    nc.vector.tensor_scalar(x_nb[:, :, S - 1:S], xb[:, :, S - 2:S - 1], 2.0, None, ALU.mult) \
                      .then_inc(dve_step, 1)
                steps[0] += 1
                s0, s1 = max(s0, 1), min(s1, S - 1)
                link(nc.vector.tensor_tensor(x_nb[:, :, s0:s1], xb[:, :, s0 - 1:s1 - 1], xb[:, :, s0 + 1:s1 + 1],
                                             ALU.add))

            def stencil_rows(b, h):
                s0, s1 = CUTS[h]
                part = poly[:, b, :, s0:s1]
                dve.wait_ge(rows_summed, NTB * b + h + 1)
                link(nc.vector.scalar_tensor_tensor(part, x_up[:, b, :, s0:s1], sc_in[:, ZX + b:ZX + b + 1], part,
                                                    ALU.mult, ALU.add))

            def stencil_last(b, h):
                if b > 0:
                    dve.wait_ge(tokens_summed, 2 * (h + 1))
                s0, s1 = h * TB, (h + 1) * TB
                nc.vector.scalar_tensor_tensor(xT[:, :, b * S + s0:b * S + s1], x_nb[:, :, s0:s1],
                                               sc_in[:, ZY + b:ZY + b + 1], poly[:, b, :, s0:s1],
                                               ALU.mult, ALU.add).then_inc(x1_done, 1)

            KK = [P, KC, KC]

            def mask_of(b):
                return blend[:, b, 0:P]

            def flag_of(b):
                return blend[:, b, P:P + KC * KC].rearrange("p (k c) -> p k c", c=KC)

            def half(h):
                return slice(h * KC // NTB, (h + 1) * KC // NTB)

            def scores_of(b, h):
                return ps[:, 4 * b + h, :].rearrange("p (k l) -> p k l", l=P)

            def masked_scores(b, h):
                dve.wait_ge(scores_ps, NTB * b + h + 1)
                link(nc.vector.tensor_tensor(probs[:, b, half(h)], scores_of(b, h),
                                             wide(mask_of(b), 1, [P, KC // NTB, P]), ALU.add))

            def maxima(b, h):
                nc.vector.tensor_reduce(chunk_max[:, b, half(h)], scores_of(b, h), AX, ALU.max) \
                  .then_inc(maxima_done, 1)
                nc.vector.tensor_reduce(inner_max[:, b, half(h)], probs[:, b, half(h)], AX, ALU.max) \
                  .then_inc(maxima_done, 1)

            def row_maxima(b):
                dve.wait_ge(maxima_done, 2 * NTB * (b + 1))
                link(nc.vector.tensor_tensor(flagged[:, b], flag_of(b), wide(chunk_max[:, b, :], 1, KK), ALU.add))
                link(nc.vector.tensor_reduce(outer_max[:, b, :], flagged[:, b], AX, ALU.max))
                link(nc.vector.tensor_tensor(row_max[:, b, :], inner_max[:, b, :], outer_max[:, b, :], ALU.max))

            def outer_exponents(b):
                dve.wait_ge(cols_ps, NTB * (b + 1))
                ex = exp_in[:, b, 0:KC * KC].rearrange("p (c k) -> p c k", k=KC)
                link(nc.vector.tensor_tensor(ex, flag_of(b).rearrange("p k c -> p c k"),
                                             wide(ps[:, COL_BANK, 0:KC], 2, KK), ALU.add))
                link(nc.vector.tensor_tensor(ex, ex, wide(outer_max[:, b, :], 1, KK), ALU.subtract))
                nc.vector.tensor_tensor(exp_in[:, b, KC * KC:], outer_max[:, b, :], row_max[:, b, :],
                                        ALU.subtract).then_inc(exps_asked, 1)

            def inner_exponents(b, h):
                nc.vector.tensor_tensor(probs[:, b, half(h)], probs[:, b, half(h)],
                                        wide(row_max[:, b, half(h)], 2, [P, KC // NTB, P]),
                                        ALU.subtract).then_inc(probs_asked, 1)

            def inner_sums(b, h):
                dve.wait_ge(probs_done, NTB * b + h + 1)
                link(nc.vector.tensor_reduce(denom[:, b, half(h)], probs[:, b, half(h)], AX, ALU.add))

            def outer_denominators(b):
                dve.wait_ge(outer_ps, b + 1)
                nc.vector.tensor_reduce(outer_sum[:, b, :], ps[:, COL_BANK, SUMS].rearrange("p (c k) -> p k c", k=KC),
                                        AX, ALU.add).then_inc(outer_read, 1)
                dve.wait_ge(outer_read, b + 1)
                link(nc.vector.tensor_tensor(outer_sum[:, b, :], outer_sum[:, b, :], exp_out[:, b, KC * KC:],
                                             ALU.mult))

            def denominators(b):
                link(nc.vector.tensor_tensor(denom[:, b, :], denom[:, b, :], outer_sum[:, b, :], ALU.add))
                link(nc.vector.tensor_tensor(denom[:, b, :], denom[:, b, :], blend[:, b, P + KC * KC:], ALU.mult))
                link(nc.vector.reciprocal(recip[:, b, :], denom[:, b, :]))

            def scaled_weights(b):
                def own(h):
                    nc.vector.tensor_tensor(probs[:, b, half(h)], probs[:, b, half(h)],
                                            wide(recip[:, b, half(h)], 2, [P, KC // NTB, P]), ALU.mult) \
                      .then_inc(probs_scaled, 1)

                nc.vector.tensor_tensor(outer_w[:, b, 0:KC], exp_out[:, b, KC * KC:], recip[:, b, :], ALU.mult) \
                  .then_inc(outer_scaled, 1)
                for group in (1, 2):
                    nc.vector.tensor_tensor(outer_w[:, b, GROUP * group:GROUP * group + KC], exp_out[:, b, KC * KC:],
                                            recip[:, b, :], ALU.mult).then_inc(outer_scaled, 1)
                own(0)
                own(1)

            def ctx_low(b):
                dve.wait_ge(ctx_hi_done, 2 * b + 2)
                nc.vector.tensor_tensor(ctx_parts[2 * GROUP:STACK, b, :], ps[0:KC, 4 * b + 3, 0:D],
                                        ctx_parts[0:KC, b, :].bitcast(f32), ALU.subtract).then_inc(ctx_done, 1)

            def outer_rows_split(b):
                dve.wait_ge(outert_ps, b + 1)
                nc.vector.tensor_copy(outer_rows[:, b, :], ps[0:STACK, 4 * b + 2, 0:P]).then_inc(rows_hi_done, 1)
                dve.wait_ge(rows_hi_done, b + 1)
                mid = slice(GROUP, GROUP + KC)
                link(nc.vector.tensor_tensor(outer_rows[mid, b, :], ps[mid, 4 * b + 2, 0:P],
                                             outer_rows[mid, b, :].bitcast(f32), ALU.subtract))

            def outer_spread(b, h):
                shape = [STACK, KC // NTB, P]
                nc.vector.tensor_tensor(outer_t[:, b, h * TB:(h + 1) * TB]
                                        .rearrange("p (k l) -> p k l", l=P),
                                        wide(outer_rows[:, b, :].bitcast(f32), 1, shape),
                                        wide(own_chunk[:, half(h)], 2, shape), ALU.mult).then_inc(outert_done, 1)

            def x_low(tb, c):
                at = tb * TB
                return nc.vector.tensor_tensor(x_lo[:, c, at:at + TB], xT[:, c, at:at + TB],
                                               x_hi[:, c, at:at + TB].bitcast(f32), ALU.subtract)

            def pooled_added(tb):
                b, h = tb // NTB, tb % NTB
                dve.wait_ge(pooled_ps, tb + 1)
                for c in range(DC):
                    xs = xT[:, c, tb * TB:(tb + 1) * TB]
                    nc.vector.tensor_tensor(xs, xs, ps[:, 4 * b + 2 * c + h, :], ALU.add).then_inc(x2_summed, 1)

            def x2_low(tb):
                for c in range(DC):
                    dve.wait_ge(x2_hi_done, DC * tb + c + 1)
                    x_low(tb, c).then_inc(x2_done, 1)

            def x3_low(tb):
                for c in range(DC):
                    dve.wait_ge(x3_hi_done, DC * tb + c + 1)
                    last = x_low(tb, c)
                last.then_inc(x3_done, 1)

            stencil_tokens(0, 0)
            stencil_square(0, 0)
            stencil_tokens(0, 1)
            stencil_rows(0, 0)
            stencil_last(0, 0)
            stencil_square(0, 1)
            stencil_rows(0, 1)
            stencil_last(0, 1)
            dve.wait_ge(masks_done, 1)
            for h in range(NTB):
                masked_scores(0, h)
                maxima(0, h)
            row_maxima(0)
            outer_exponents(0)
            inner_exponents(0, 0)
            inner_exponents(0, 1)
            outer_denominators(0)
            inner_sums(0, 0)
            inner_sums(0, 1)
            denominators(0)
            scaled_weights(0)
            outer_rows_split(0)
            ctx_low(0)
            outer_spread(0, 0)
            outer_spread(0, 1)
            gates()
            pooled_added(0)
            x2_low(0)
            pooled_added(1)
            x2_low(1)

            between = {(0, 0): [lambda: stencil_square(1, 0)],
                       (0, 1): [lambda: stencil_rows(1, 0)],
                       (0, 2): [lambda: stencil_last(1, 0)],
                       (0, 3): [lambda: stencil_square(1, 1)],
                       (0, 4): [lambda: stencil_rows(1, 1)],
                       (0, 5): [lambda: stencil_last(1, 1)],
                       (1, 0): [lambda: masked_scores(1, 0), lambda: maxima(1, 0)],
                       (1, 1): [lambda: masked_scores(1, 1), lambda: maxima(1, 1), lambda: row_maxima(1)],
                       (1, 2): [lambda: outer_exponents(1), lambda: inner_exponents(1, 0),
                                lambda: inner_exponents(1, 1)],
                       (1, 3): [lambda: x3_low(0)],
                       (1, 4): [lambda: outer_denominators(1), lambda: inner_sums(1, 0),
                                lambda: inner_sums(1, 1), lambda: denominators(1)],
                       (1, 5): [lambda: scaled_weights(1)],
                       (1, 6): [lambda: ctx_low(1)],
                       (1, 7): [lambda: outer_rows_split(1), lambda: outer_spread(1, 0), lambda: outer_spread(1, 1),
                                lambda: pooled_added(2), lambda: x2_low(2)],
                       (2, 1): [lambda: pooled_added(3)],
                       (2, 2): [lambda: x2_low(3)],
                       (2, 4): [lambda: x3_low(1)],
                       (3, 2): [lambda: x3_low(2)]}

            def weight_piece(slot, tb, i, done):
                at = tb * WQ + i * WP
                dve.wait_ge(whi_done, done)
                nc.vector.tensor_tensor(w_lo[slot][:, ds(at, WP)], raw[:, ds(at, WP)],
                                        w_hi[slot][:, ds(at, WP)].bitcast(f32), ALU.subtract).then_inc(wlo_done, 1)

            for tb in range(NT):
                b = tb // NTB
                for k in range(FC):
                    n = FC * tb + k
                    dve.wait_ge(fc_hi_done, n + 1)
                    nc.vector.tensor_tensor(h_lo[:, k % RING, :], stage[:, n % PAIR, :],
                                            h_hi[:, k % RING, :].bitcast(f32), ALU.subtract).then_inc(fc_h_ready, 1)
                    for stage_of_1 in between.get((tb, k), []):
                        stage_of_1()
                    if tb >= NTB:
                        at = (tb - NTB) * FC + k
                        weight_piece(1, at // PIECES, at % PIECES, at + 1)
                dve.wait_ge(down_done, RING + FC * (tb + 1))
                for c in range(DC):
                    xs = xT[:, c, tb * TB:(tb + 1) * TB]
                    nc.vector.scalar_tensor_tensor(xs, ps[:, FC_OUT + c, :], out_bias[:, b, c:c + 1], xs,
                                                   ALU.add, ALU.add).then_inc(fc_summed, 1)
            x3_low(NT - 1)

            def expert_block(e, slot, tb, split):
                for k in range(FC):
                    n = e * (NT * FC) + tb * FC + k
                    dve.wait_ge(silu_done, n + 1)
                    nc.vector.scalar_tensor_tensor(hidden[:, k % PAIR, :], stage[:, k % PAIR, :],
                                                   gate[:, ds(e, 1), ds(tb, 1)].rearrange("p e t -> p (e t)"),
                                                   ps[:, PAIR_BANK[k % PAIR] + 1, :], ALU.mult, ALU.mult) \
                      .then_inc(mul_done, 1)
                    dve.wait_ge(down_done, NT * FC + n + 1)
                    dve.wait_ge(mul_done, PAIR + n + 1)
                    nc.vector.tensor_copy(h_hi[:, k % RING, :], hidden[:, k % PAIR, :]).then_inc(hi_done, 1)
                    dve.wait_ge(hi_done, n + 1)
                    nc.vector.tensor_tensor(h_lo[:, k % RING, :], hidden[:, k % PAIR, :],
                                            h_hi[:, k % RING, :].bitcast(f32), ALU.subtract).then_inc(h_ready, 1)
                    if split and k % 2 == 1:
                        weight_piece(1 - slot, tb, k // 2,
                                     (e + 1) * (NT * PIECES) + tb * PIECES + k // 2 + 1)
                dve.wait_ge(down_done, RING + NT * FC + (e * NT + tb + 1) * FC)
                for c in range(DC):
                    xs = xT[:, c, ds(tb * TB, TB)]
                    nc.vector.tensor_tensor(xs, xs, ps[:, OUT + c, :], ALU.add).then_inc(out_free, 1)

            def expert(e, slot, split):
                with dve.Fori(0, NT) as tb:
                    expert_block(e, slot, tb, split)

            with dve.Fori(0, EG // 2) as pair:
                expert(pair * 2, 1, True)
                expert(pair * 2 + 1, 0, True)
            expert(EG, 1, False)

        @block.tensor
        def _(pe):
            def mm(out_ap, lhsT, rhs, first, last):
                return nc.tensor.matmul(out_ap, lhsT, rhs, start=first, stop=last)

            def score_layer(b, h):
                pe.wait_ge(x1_done, b * NTB + h + 1)
                for c in range(DC):
                    last = mm(ps[0:A, 4 * b + h, :], w1_sb[:, c, :], xT[:, c, b * S + h * TB:b * S + (h + 1) * TB],
                              c == 0, c == DC - 1)
                last.then_inc(attn_ps, 1)

            def to_tokens(b, r):
                if r == 1 and TOK_BANK[b][1] == TOK_BANK[b][0]:
                    pe.wait_ge(tok_done, 2 * b + 1)
                for k in range(KC // 2):
                    for c in range(DC):
                        at = k * D + c * P
                        s0 = b * S + (r * KC // 2 + k) * P
                        last = nc.tensor.transpose(ps[:, TOK_BANK[b][r] + at // TB, at % TB:at % TB + P],
                                                   xT[:, c, s0:s0 + P], ident[:, :])
                last.then_inc(tok_ps, 1)

            def scores(b, h):
                pe.wait_ge(attn_done, NTB * b + h + 1)
                mm(ps[:, 4 * b + h, :], v_wide[:, :], attn[:, b, h * TB:(h + 1) * TB], True, True) \
                  .then_inc(scores_ps, 1)

            def score_columns(b, h):
                if COL_BANK in TOK_BANK[b]:
                    pe.wait_ge(tok_done, 2 * b + 2)
                for k in range(h * KC // NTB, (h + 1) * KC // NTB):
                    last = mm(ps[:, COL_BANK, k:k + 1], attn[:, b, k * P:(k + 1) * P], v_sb[:, 0:1], True, True)
                last.then_inc(cols_ps, 1)

            def outer_sums(b):
                pe.wait_ge(exps_done, b + 1)
                mm(ps[:, COL_BANK, SUMS], ones[:, :], exp_out[:, b, 0:KC * KC], True, True).then_inc(outer_ps, 1)
                for c in range(KC):
                    if c % (KC // 2) == 0:
                        pe.wait_ge(tok_done, 2 * b + 2 * c // KC + 1)
                    last = mm(ps[0:KC, 4 * b + 3, 0:D], exp_out[:, b, c * KC:(c + 1) * KC], x_tok[:, b, c, :],
                              c == 0, c == KC - 1)
                last.then_inc(ctx_ps, 1)

            def outer_transposed(b):
                pe.wait_ge(outer_scaled, 3 * (b + 1))
                nc.tensor.transpose(ps[0:STACK, 4 * b + 2, 0:P], outer_w[:, b, :], ident[:, :]).then_inc(outert_ps, 1)

            def weights_transposed(b, h):
                pe.wait_ge(probs_scaled, NTB * b + h + 1)
                for i in range(KC // NTB):
                    last = nc.tensor.transpose(ps[:, 4 * b + h, i * P:(i + 1) * P],
                                               probs[:, b, h * KC // NTB + i, :], ident[:, :])
                last.then_inc(probst_ps, 1)

            def pooled(b, h):
                pe.wait_ge(probst_done, NTB * b + h + 1)
                pe.wait_ge(outert_done, NTB * b + h + 1)
                pe.wait_ge(ctx_done, b + 1)
                for c in range(DC):
                    bank = ps[:, 4 * b + 2 * c + h, :]
                    mm(bank, ctx_parts[:, b, c * P:(c + 1) * P],
                       outer_t[:, b, h * TB:(h + 1) * TB], True, False)
                    for i in range(TB // P):
                        k = h * (TB // P) + i
                        last = mm(bank[:, i * P:(i + 1) * P], x_tok[:, b, k, c * P:(c + 1) * P],
                                  probs_t[:, b, k, :], False, i == TB // P - 1)
                last.then_inc(pooled_ps, 1)

            def keep_warm(n):
                for _ in range(n):
                    mm(ps[:, 7, 0:P], ident[:, :], ident[:, :], True, True)

            pe.wait_ge(consts_done, 1)
            pe.wait_ge(x_in[0][0], 16)
            keep_warm(WARM[0])
            pe.wait_ge(w1_in, 48)
            score_layer(0, 0)
            pe.wait_ge(v_done, 1)
            keep_warm(WARM[1])
            scores(0, 0)
            score_layer(0, 1)
            score_columns(0, 0)
            scores(0, 1)
            score_columns(0, 1)
            to_tokens(0, 0)
            to_tokens(0, 1)
            outer_sums(0)
            outer_transposed(0)
            weights_transposed(0, 0)
            weights_transposed(0, 1)
            pooled(0, 0)
            pooled(0, 1)

            between = {(0, 4): [lambda: score_layer(1, 0)],
                       (0, 5): [lambda: to_tokens(1, 0)],
                       (0, 6): [lambda: scores(1, 0)],
                       (0, 7): [lambda: score_layer(1, 1)],
                       (1, 0): [lambda: scores(1, 1)],
                       (1, 1): [lambda: to_tokens(1, 1)],
                       (1, 2): [lambda: score_columns(1, 0), lambda: score_columns(1, 1)],
                       (1, 4): [lambda: outer_sums(1)],
                       (1, 7): [lambda: outer_transposed(1), lambda: weights_transposed(1, 0),
                                lambda: weights_transposed(1, 1)]}

            def split_mm(out_ap, parts, first, last):
                (wh, wl), (xh, xl) = parts
                mm(out_ap, wh, xh, first, False)
                mm(out_ap, wh, xl, False, False)
                return mm(out_ap, wl, xh, False, last)

            def up(tile_at, bank, k, tokens, split_before=None):
                for c in range(DC):
                    if split_before is not None:
                        pe.wait_ge(x2_done, split_before + c + 1)
                    at = tile_at[1] + c * F + k * P
                    hi, lo = w_hi[tile_at[0]], w_lo[tile_at[0]]
                    last = split_mm(ps[:, bank, :], ((hi[:, at:at + P], lo[:, at:at + P]),
                                                     (x_hi[:, c, tokens], x_lo[:, c, tokens])), c == 0, c == DC - 1)
                return last

            def down(weights, bank, k):
                for c in range(DC):
                    wh, wl = weights(c, k)
                    last = split_mm(ps[:, bank + c, :], ((wh, wl), (h_hi[:, k % RING, :], h_lo[:, k % RING, :])),
                                    k == 0, k == FC - 1)
                return last

            ORDER = [("up", 0), ("up", 1)]
            for k in range(FC - 3):
                ORDER += [("up", k + 2), ("down", k)]
            ORDER[-1:] = []
            ORDER += [("up", FC - 1)] + [("down", k) for k in range(FC - 4, FC)]

            pe.wait_ge(fc_split, UP // FCP)
            for tb in range(NT):
                b = tb // NTB
                for kind, k in ORDER:
                    n = FC * tb + k
                    if kind == "up":
                        if n == 1:
                            pe.wait_ge(x2_summed, NT)
                        pe.wait_ge(gelu_done, n + 1)
                        up((0, 0), n % PAIR, k, ds(tb * TB, TB), DC * tb if k == 0 else None).then_inc(fc_up, 1)
                        for stage_of_1 in between.get((tb, k), []):
                            stage_of_1()
                    else:
                        if k == 0:
                            pe.wait_ge(fc_split, UP // FCP + 2 + b)
                            if tb > 0:
                                pe.wait_ge(fc_summed, DC * tb)
                        pe.wait_ge(fc_h_ready, PAIR + n + 1)
                        last = down(lambda c, k: (fc2_cols(w_hi[0], b, c)[:, k, :], fc2_cols(w_lo[0], b, c)[:, k, :]),
                                    FC_OUT, k)
                        last.then_inc(down_done, 1)
                        if tb == 1 and k == FC - 2:
                            pooled(1, 0)
                            pooled(1, 1)

            def expert_block(e, slot, tb):
                def weights(c, k):
                    at = 2 * UP + k * D + c * P
                    return w_hi[slot][:, at:at + P], w_lo[slot][:, at:at + P]

                for kind, k in ORDER:
                    n = e * (NT * FC) + tb * FC + k
                    if kind == "up":
                        pe.wait_ge(mul_done, n + 1)
                        up((slot, 0), PAIR_BANK[k % PAIR], k, ds(tb * TB, TB))
                        up((slot, UP), PAIR_BANK[k % PAIR] + 1, k, ds(tb * TB, TB)).then_inc(up_done, 1)
                    else:
                        if k == 0:
                            pe.wait_ge(out_free, (e * NT + tb + 1) * DC)
                        pe.wait_ge(h_ready, n + 1)
                        down(weights, OUT, k).then_inc(down_done, 1)

            pe.wait_ge(gelu_done, PAIR + NT * FC)

            def expert(e, slot):
                with pe.Fori(0, NT) as tb:
                    pe.wait_ge(wlo_done, (e + 1) * (NT * PIECES))
                    pe.wait_ge(x3_done, tb + 1)
                    expert_block(e, slot, tb)

            with pe.Fori(0, EG // 2) as pair:
                expert(pair * 2, 1)
                expert(pair * 2 + 1, 0)
            expert(EG, 1)


def kernel(x, condB_zX, condB_zY, condB_zR, itok_B_0_2, itok_B_0_15, fside_Bx8_0, condB_sharedgateprob,
           L1_cond_W1, L1_cond_b1, L1_cond_v, L2_cond_fc1_w, L2_cond_fc1_b, L2_cond_fc2_w, L2_cond_fc2_b,
           L2_cond_experts_w, L2_cond_experts_b, L3_cond_Wg, L3_cond_Wu, L3_cond_Wd, L3_cond_Sg, L3_cond_Su,
           L3_cond_Sd):
    import numpy as np
    import concourse.bacc as bacc
    from concourse.bass_utils import run_bass_kernel_spmd

    P = 128

    def rows_of(w):
        w = np.asarray(w)
        return np.moveaxis(w.reshape(*w.shape[:-2], w.shape[-2] // P, P, w.shape[-1]), -3, -2)

    def flat(w):
        return w.reshape(*w.shape[:-2], -1)

    x = np.asarray(x)
    D = x.shape[2]
    reflected = [1, *range(D), D - 2]
    moe = [flat(rows_of(np.concatenate([routed, np.asarray(shared)[None]])))
           for routed, shared in ((L3_cond_Wg, L3_cond_Sg), (L3_cond_Wu, L3_cond_Su), (L3_cond_Wd, L3_cond_Sd))]
    arrays = {
        "x_rows": x.transpose(2, 0, 1)[reflected],
        "scalars": np.concatenate([np.asarray(a).ravel() for a in
                                   (condB_zX, condB_zY, condB_zR, condB_sharedgateprob, fside_Bx8_0)]),
        "types": np.asarray(itok_B_0_2),
        "expert_ids": np.asarray(itok_B_0_15),
        "w1": np.asarray(L1_cond_W1),
        "b1": np.asarray(L1_cond_b1),
        "v": np.asarray(L1_cond_v),
        "fc1_w": rows_of(np.asarray(L2_cond_fc1_w).T),
        "fc1_b": np.asarray(L2_cond_fc1_b).reshape(-1, P).T,
        "fc2_w": rows_of(np.asarray(L2_cond_fc2_w).T),
        "fc2_b": np.asarray(L2_cond_fc2_b),
        "experts_w": rows_of(np.asarray(L2_cond_experts_w).transpose(0, 2, 1)),
        "experts_b": np.asarray(L2_cond_experts_b),
        "moe_w": np.concatenate(moe, axis=-1),
    }
    nc = bacc.Bacc("TRN2", target_bir_lowering=False, num_devices=1)
    args, given = [], {}
    for name, a in arrays.items():
        given[f"in_{name}"] = np.ascontiguousarray(a)
        args.append(nc.dram_tensor(f"in_{name}", a.shape, mybir.dt.from_np(a.dtype), kind="ExternalInput").ap())
    B, S, _ = x.shape
    args.append(nc.dram_tensor("out_x", (D, B * S), mybir.dt.float32, kind="ExternalOutput").ap())
    stencil_attention_experts(nc, *args)
    r = run_bass_kernel_spmd(nc, [given], core_ids=[0])
    return np.ascontiguousarray(r.results[0]["out_x"].reshape(D, B, S).transpose(1, 2, 0))
```
